# Optimizing a Trainium2 kernel written in Bass

```python
import numpy as np
import jax
import jax.numpy as jnp

def _softmax(x, axis=-1):
    return jax.nn.softmax(x, axis=axis)

def _gelu(x):
    return jax.nn.gelu(x, approximate=True)

def _silu(x):
    return jax.nn.silu(x)

def _sigmoid(x):
    return jax.nn.sigmoid(x)

def _layernorm(x, axis=-1, eps=1e-05):
    m = jnp.mean(x, axis=axis, keepdims=True)
    v = jnp.var(x, axis=axis, keepdims=True)
    return (x - m) / jnp.sqrt(v + eps)

def _scatter_add(tgt, idx, src, axis=0):
    return tgt.at[idx].add(src)

def _segment_sum(src, seg, n):
    return jax.ops.segment_sum(src, seg, n)
kernel_name = 'mk_macaron_d1_jaxref_r4_ed0a50'

def setup_inputs(seed: int=0):
    np.random.seed(seed)
    _w = jnp.asarray

    def _L0_attn_setup():
        import jax, jax.numpy as jnp
        import numpy as np
        B, T, D = (4, 512, 256)
        H, DK = (8, 64)
        EPS = 1e-06

        def _xavier(key, shape):
            fan_in, fan_out = (shape[1], shape[0])
            lim = float(np.sqrt(6.0 / (fan_in + fan_out)))
            return jax.random.uniform(key, shape, jnp.float32, -lim, lim)

        def _phi(u):
            return jax.nn.elu(u) + 1.0
        key = jax.random.key(seed)
        ks = jax.random.split(key, 7)
        x = jax.random.normal(ks[0], (B, T, D), jnp.float32)
        W_Q = _xavier(ks[1], (H * DK, D))
        W_K = _xavier(ks[2], (H * DK, D))
        W_V = _xavier(ks[3], (H * DK, D))
        W_g_w = _xavier(ks[4], (H * DK, D))
        W_g_b = jax.random.normal(ks[5], (H * DK,), jnp.float32) * 0.02
        W_O = _xavier(ks[6], (D, H * DK))
        decay_log = jnp.zeros((H,), jnp.float32)
        return {'x': x, 'W_Q': W_Q, 'W_K': W_K, 'W_V': W_V, 'W_g_w': W_g_w, 'W_g_b': W_g_b, 'W_O': W_O, 'decay_log': decay_log}
    _L0_attn_in = _L0_attn_setup()

    def _L0_ffn_setup():
        import jax, jax.numpy as jnp
        import numpy as np
        DIM = 256

        def _reference_tuple_inner(x, W_r, W_k, W_v, mu_r, mu_k):
            B, T, C = x.shape
            x_prev = jnp.concatenate([jnp.zeros((B, 1, C), x.dtype), x[:, :-1, :]], axis=1)
            xr = mu_r * x + (1.0 - mu_r) * x_prev
            xk = mu_k * x + (1.0 - mu_k) * x_prev
            r = jax.nn.sigmoid(jnp.einsum('btc,dc->btd', xr, W_r))
            k = jnp.einsum('btc,dc->btd', xk, W_k)
            k_act = jnp.square(jax.nn.relu(k))
            out = r * jnp.einsum('btc,dc->btd', k_act, W_v)
            new_state = x[:, -1, :]
            return (out, new_state)
        key = jax.random.key(seed)
        ks = jax.random.split(key, 6)
        B, T, C = (8, 512, DIM)
        x = jax.random.normal(ks[0], (B, T, C), dtype=jnp.float32)
        s = 1.0 / np.sqrt(C)
        W_r = jax.random.uniform(ks[1], (C, C), jnp.float32, -s, s)
        W_k = jax.random.uniform(ks[2], (C, C), jnp.float32, -s, s)
        W_v = jax.random.uniform(ks[3], (C, C), jnp.float32, -s, s)
        mu_r = jax.random.uniform(ks[4], (C,), jnp.float32)
        mu_k = jax.random.uniform(ks[5], (C,), jnp.float32)
        return {'x': x, 'W_r': W_r, 'W_k': W_k, 'W_v': W_v, 'mu_r': mu_r, 'mu_k': mu_k}
    _L0_ffn_in = _L0_ffn_setup()
    _d = {'L0_attn_x': _L0_attn_in['x'], 'L0_attn_W_Q': _L0_attn_in['W_Q'], 'L0_attn_W_K': _L0_attn_in['W_K'], 'L0_attn_W_V': _L0_attn_in['W_V'], 'L0_attn_W_g_w': _L0_attn_in['W_g_w'], 'L0_attn_W_g_b': _L0_attn_in['W_g_b'], 'L0_attn_W_O': _L0_attn_in['W_O'], 'L0_attn_decay_log': _L0_attn_in['decay_log'], 'L0_ffn_W_r': _L0_ffn_in['W_r'], 'L0_ffn_W_k': _L0_ffn_in['W_k'], 'L0_ffn_W_v': _L0_ffn_in['W_v'], 'L0_ffn_mu_r': _L0_ffn_in['mu_r'], 'L0_ffn_mu_k': _L0_ffn_in['mu_k']}
    _x0 = _d['L0_attn_x']
    _d['L0_attn_x'] = jax.random.normal(jax.random.fold_in(jax.random.key(seed), 1), (8, 1024, 256), dtype=_x0.dtype)
    del _x0
    return _d

def reference(L0_attn_x, L0_attn_W_Q, L0_attn_W_K, L0_attn_W_V, L0_attn_W_g_w, L0_attn_W_g_b, L0_attn_W_O, L0_attn_decay_log, L0_ffn_W_r, L0_ffn_W_k, L0_ffn_W_v, L0_ffn_mu_r, L0_ffn_mu_k):

    def _L0_attn_ref(x, W_Q, W_K, W_V, W_g_w, W_g_b, W_O, decay_log):
        import jax, jax.numpy as jnp
        import numpy as np
        B, T, D = (4, 512, 256)
        H, DK = (8, 64)
        EPS = 1e-06

        def _xavier(key, shape):
            fan_in, fan_out = (shape[1], shape[0])
            lim = float(np.sqrt(6.0 / (fan_in + fan_out)))
            return jax.random.uniform(key, shape, jnp.float32, -lim, lim)

        def _phi(u):
            return jax.nn.elu(u) + 1.0
        b, t, d = x.shape
        q = _phi((x @ W_Q.T).reshape(b, t, H, DK))
        k = _phi((x @ W_K.T).reshape(b, t, H, DK))
        v = (x @ W_V.T).reshape(b, t, H, DK)
        gamma = jax.nn.sigmoid(decay_log)
        g4 = gamma[None, :, None, None]
        g3 = gamma[None, :, None]
        qT = jnp.moveaxis(q, 1, 0)
        kT = jnp.moveaxis(k, 1, 0)
        vT = jnp.moveaxis(v, 1, 0)
        S0 = jnp.zeros((b, H, DK, DK), x.dtype)
        z0 = jnp.zeros((b, H, DK), x.dtype)

        def step(carry, inp):
            S, z = carry
            qt, kt, vt = inp
            S = g4 * S + jnp.einsum('bhi,bhj->bhij', kt, vt)
            z = g3 * z + kt
            num = jnp.einsum('bhij,bhi->bhj', S, qt)
            den = jnp.sum(z * qt, axis=-1, keepdims=True) + EPS
            return ((S, z), num / den)
        _, ys = jax.lax.scan(step, (S0, z0), (qT, kT, vT))
        outputs = jnp.moveaxis(ys, 0, 1)
        gate = jax.nn.sigmoid(x @ W_g_w.T + W_g_b).reshape(b, t, H, DK)
        y = (outputs * gate).reshape(b, t, H * DK)
        return y @ W_O.T

    def _L0_ffn_ref(x, W_r, W_k, W_v, mu_r, mu_k):
        import jax, jax.numpy as jnp
        import numpy as np
        DIM = 256

        def _reference_tuple_inner(x, W_r, W_k, W_v, mu_r, mu_k):
            B, T, C = x.shape
            x_prev = jnp.concatenate([jnp.zeros((B, 1, C), x.dtype), x[:, :-1, :]], axis=1)
            xr = mu_r * x + (1.0 - mu_r) * x_prev
            xk = mu_k * x + (1.0 - mu_k) * x_prev
            r = jax.nn.sigmoid(jnp.einsum('btc,dc->btd', xr, W_r))
            k = jnp.einsum('btc,dc->btd', xk, W_k)
            k_act = jnp.square(jax.nn.relu(k))
            out = r * jnp.einsum('btc,dc->btd', k_act, W_v)
            new_state = x[:, -1, :]
            return (out, new_state)
        return _reference_tuple_inner(x, W_r, W_k, W_v, mu_r, mu_k)[0]
    x = L0_attn_x
    x = x + 0.5 * _L0_ffn_ref(_layernorm(x, axis=-1), L0_ffn_W_r, L0_ffn_W_k, L0_ffn_W_v, L0_ffn_mu_r, L0_ffn_mu_k)
    x = x + _L0_attn_ref(_layernorm(x, axis=-1), L0_attn_W_Q, L0_attn_W_K, L0_attn_W_V, L0_attn_W_g_w, L0_attn_W_g_b, L0_attn_W_O, L0_attn_decay_log)
    x = x + 0.5 * _L0_ffn_ref(_layernorm(x, axis=-1), L0_ffn_W_r, L0_ffn_W_k, L0_ffn_W_v, L0_ffn_mu_r, L0_ffn_mu_k)
    return x

_drawn_inputs = setup_inputs


def setup_inputs(seed=0):
    import zlib

    import numpy as np

    out = dict(_drawn_inputs(seed))
    spreads = {'L0_attn_decay_log': (0.0, 0.8)}
    factors = {'L0_attn_W_Q': 6.768,
     'L0_attn_W_K': 3.426,
     'L0_attn_W_g_b': 22.043,
     'L0_ffn_W_r': 3.311,
     'L0_ffn_mu_r': 6.731}
    for name, (base, spread) in spreads.items():
        noise = np.random.default_rng([zlib.crc32(name.encode()), seed]).standard_normal(out[name].shape)
        drawn = base * np.exp(spread * noise) if base else spread * noise
        out[name] = jnp.asarray(drawn.astype(out[name].dtype))
    for name, factor in factors.items():
        out[name] = (out[name] * factor).astype(out[name].dtype)
    return out
```

```python
from contextlib import ExitStack

import concourse.bass as bass
from concourse import mybir

F32 = mybir.dt.float32
F32R = mybir.dt.float32r
ACT = mybir.ActivationFunctionType
ALU = mybir.AluOpType

P = 128
CH = 4
GT = CH * P
RING = 4
LN_EPS = 1e-5
DEN_EPS = 1e-6

OFF_RING = ("qk", "num", "o_half")
ORDER = (
    [("B", "xt", 0), ("B", "xt", 1), ("A", "xt", 0), ("A", "xt", 1)]
    + [("B", "q", d) for d in range(4)] + [("B", "k", d) for d in range(4)]
    + [("A", "k", 0), ("A", "k", 1), ("A", "r", 0), ("A", "r", 1)]
    + [("B", "v", 0), ("B", "kt", 0), ("B", "qk", 0), ("B", "g", 0)]
    + [("C", "xt", 0), ("C", "xt", 1), ("B", "v", 1), ("A", "kv", 0), ("A", "kv", 1)]
    + [("B", "kt", 1), ("B", "qk", 1), ("B", "g", 1), ("B", "s", 0), ("B", "s", 1), ("B", "num", 0)]
    + [("C", "k", 0), ("C", "k", 1), ("B", "yt", 0), ("B", "v", 2), ("B", "kt", 2), ("B", "qk", 2)]
    + [("B", "g", 2), ("B", "s", 2), ("B", "s", 3), ("B", "num", 1), ("C", "r", 0), ("C", "r", 1)]
    + [("B", "yt", 1), ("B", "v", 3), ("B", "o", 0), ("B", "kt", 3), ("B", "qk", 3)]
    + [("B", "g", 3), ("B", "s", 4), ("B", "s", 5), ("B", "num", 2), ("B", "yt", 2)]
    + [("B", "s", 6), ("B", "s", 7), ("B", "num", 3), ("C", "kv", 0), ("C", "kv", 1)]
    + [("B", "yt", 3), ("B", "o", 1)]
)
LAG = {"A": 0, "B": 1, "C": 2}


def tiles_of(stages):
    return [t for t in ORDER if t[0] in stages and t[1] not in OFF_RING]


def macaron(nc, x, W_Q, W_K, W_V, W_G, b_G, W_O, decay_log, W_r, W_k, W_v, mu_r, mu_k, out):
    B, T, D = x.shape
    HD = W_Q.shape[0]
    H = decay_log.shape[0]
    DK = HD // H
    KT = D // P
    PT = HD // P
    V1 = DK + 1
    N = B * T // GT
    assert T == 2 * GT and D == 2 * P and HD == 4 * P and DK == 64 and H == 8

    stages_at = [[s for s in "ABC" if 0 <= i - LAG[s] < N] for i in range(N + 2)]
    full = len(tiles_of("ABC"))
    assert full % RING == 0 and all(sum(len(tiles_of(s)) for s in stages_at[:i]) % RING == 0 for i in range(5))

    x_g = x.rearrange("b (g c p) d -> (b g) p c d", c=CH, p=P)
    out_g = out.rearrange("b (g c p) d -> (b g) p c d", c=CH, p=P)

    with ExitStack() as ctx:
        def sb(name, shape, dt=F32):
            return ctx.enter_context(nc.sbuf_tensor(name, shape, dt))

        def sem(name):
            return ctx.enter_context(nc.semaphore(name))

        ring = [ctx.enter_context(nc.psum_tensor(f"ring{b}", [P, GT], F32)) for b in range(RING)]
        ps_qk = [ctx.enter_context(nc.psum_tensor(f"ps_qk{b}", [P, 4, P], F32)) for b in range(2)]
        ps_num = [ctx.enter_context(nc.psum_tensor(f"ps_num{b}", [P, 512], F32)) for b in range(2)]

        ident = sb("ident", [P, P])
        zeros = sb("zeros", [P, P])
        m_half = sb("m_half", [P, CH])
        ln_eps = sb("ln_eps", [P, CH])
        spare = sb("spare", [P, 1])
        gl = sb("gl", [P, H])
        gpl = sb("gpl", [P, PT])
        gam = sb("gam", [P, H])
        gamp = sb("gamp", [P, PT])
        dmask = sb("dmask", [P, H, P])
        qdec = sb("qdec", [P, PT, P])
        bias = sb("bias", [P, HD])
        mur = sb("mur", [P, KT])
        muk = sb("muk", [P, KT])
        wnames = {"q": (W_Q, KT, HD), "k": (W_K, KT, HD), "v": (W_V, KT, HD), "g": (W_G, KT, HD),
                  "o": (W_O, PT, D), "fr": (W_r, KT, D), "fk": (W_k, KT, D), "fv": (W_v, KT, D)}
        wh = {n: sb(f"wh_{n}", [P, k, m], F32R) for n, (_, k, m) in wnames.items()}
        wl = {n: sb(f"wl_{n}", [P, k, m], F32R) for n, (_, k, m) in wnames.items()}

        xin = sb("xin", [P, CH, D])
        x1 = [sb(f"x1_{p}", [P, CH, D]) for p in range(2)]
        x2 = [sb(f"x2_{p}", [P, CH, D]) for p in range(2)]

        st_f, mv_f, rs_f, xn_f = sb("st_f", [P, CH, 6]), sb("mv_f", [P, CH, 2]), sb("rs_f", [P, CH]), sb("xn_f", [P, CH, D])
        xt = {s: sb(f"xt_{s}", [P, KT, 1 + GT]) for s in "AC"}
        dx = sb("dx", [P, KT, GT])
        mix = {m: sb(f"mix_{m}", [P, KT, GT]) for m in "kr"}
        mixh = {m: sb(f"mixh_{m}", [P, KT, GT], F32R) for m in "kr"}
        mixl = {m: sb(f"mixl_{m}", [P, KT, GT], F32R) for m in "kr"}
        kr, ks, ksh, ksl = dx, mix["k"], mixh["k"], mixl["k"]
        rsig = fo = mix["r"][:, :, :].rearrange("p k (c d) -> p (k c) d", d=D)

        st_b, mv_b, rs_b, xn_b = sb("st_b", [P, CH, 6]), sb("mv_b", [P, CH, 2]), sb("rs_b", [P, CH]), sb("xn_b", [P, CH, D])
        xth = sb("xth", [P, KT, GT], F32R)
        xtl = sb("xtl", [P, KT, GT], F32R)
        ex = [sb(f"ex{b}", [P, GT]) for b in range(2)]
        qt = sb("qt", [P, PT, GT])
        qd = [sb(f"qd{b}", [P, PT, P]) for b in range(2)]
        kt = sb("kt", [P, PT, GT])
        kpad = [sb(f"kpad{e}", [P, PT, GT]) for e in range(2)]
        vv = sb("vv", [P, 2, H, V1])
        gate = sb("gate", [P, 2, HD])
        kd = [sb(f"kd{b}", [P, HD]) for b in range(2)]
        at = [sb(f"at{b}", [P, H, P]) for b in range(2)]
        stage = [b[:, :, :].rearrange("p h t -> p (h t)") for b in at]
        S = [sb(f"S{b}", [P, PT, 2 * V1]) for b in range(2)]
        den = sb("den", [P, H])
        rden = sb("rden", [P, H])
        y = sb("y", [P, HD])
        yh = [sb(f"yh{b}", [P, PT, P], F32R) for b in range(2)]
        yl = [sb(f"yl{b}", [P, PT, P], F32R) for b in range(2)]

        s_const, s_dmac, s_setup = sem("s_const"), sem("s_dmac"), sem("s_setup")
        s_wload = [sem(f"s_wload{b}") for b in range(2)]
        s_wt, s_wh, s_wl = sem("s_wt"), sem("s_wh"), sem("s_wl")
        s_gam, s_carry, s_neg = sem("s_gam"), sem("s_carry"), sem("s_neg")
        s_x = sem("s_x")
        s_out = [sem(f"s_out{p}") for p in range(2)]
        ready = [sem(f"ring_ready{b}") for b in range(RING)]
        free = [sem(f"ring_free{b}") for b in range(RING)]
        s_stat, s_var, s_rv, s_rstd, s_xn = [{k: sem(f"s_{n}_{k}") for k in "fb"} for n in ("stat", "var", "rv", "rstd", "xn")]
        s_xt, s_dx, s_mix = sem("s_xt"), sem("s_dx"), {m: sem(f"s_mix_{m}") for m in "kr"}
        s_mixh, s_mixl = {m: sem(f"s_mixh_{m}") for m in "kr"}, {m: sem(f"s_mixl_{m}") for m in "kr"}
        s_kr, s_ks, s_ksh, s_ksl, s_rsig, s_fo, s_res = [sem("s_" + n) for n in ("kr", "ks", "ksh", "ksl", "rsig", "fo", "res")]
        s_xth, s_xtl, s_ex, s_phi, s_kpad, s_qd = [sem("s_" + n) for n in ("xth", "xtl", "ex", "phi", "kpad", "qd")]
        s_vv, s_gpre, s_gate, s_kd, s_qk, s_at = [sem("s_" + n) for n in ("vv", "gpre", "gate", "kd", "qk", "at")]
        s_S, s_num, s_den, s_rden, s_y, s_yh, s_yl, s_x2 = [sem("s_" + n) for n in ("S", "num", "den", "rden", "y", "yh", "yl", "x2")]

        class Step:

            def __init__(self, j, c, typical):
                self.j, self.c = j, c
                self.stages = stages_at[typical]
                self.before = typical

            def g(self, stage, ahead=0):
                k = self.c + ahead - LAG[stage]
                return 2 * self.j + k, k % 2, self.j + k // 2

            def job(self, stage):
                i = 2 * self.j + self.c
                if isinstance(i, int) and i < 2:
                    return i
                if isinstance(i, int) and i >= N:
                    return 2 * N - 2 + i - N
                return 2 * i - (2 if stage == "A" else 1)

            def tile(self, stage, kind, n):
                done = sum(len(tiles_of(s)) for s in stages_at[:self.c])
                at = done + tiles_of(self.stages).index((stage, kind, n))
                return at % RING, 2 * (full // RING) * self.j + at // RING + 1

            def tile_before(self, stage, kind, n):
                at = tiles_of(self.stages).index((stage, kind, n)) - RING
                if at >= 0:
                    return self, tiles_of(self.stages)[at]
                if self.c == 0:
                    return None
                last = Step(self.j, self.c - 1, self.before - 1 if isinstance(self.j, int) else self.before)
                return last, tiles_of(last.stages)[at]

            def has(self, stage):
                return stage in self.stages

        def filled(step, stage, kind, n):
            b, count = step.tile(stage, kind, n)
            return ready[b], count

        def released(step, stage, kind, n):
            if stage == "B":
                g, _, _ = step.g("B")
                s, per = {"xt": (s_xtl, 2), "q": (s_phi, 8), "k": (s_phi, 8), "v": (s_vv, 4), "g": (s_gpre, 4),
                          "kt": (s_kd, 4), "s": (s_S, 8), "yt": (s_yl, 4), "o": (s_x2, 2)}[kind]
                return s, per * g + n + 1 + (4 if kind == "k" else 0)
            s = {"xt": s_xt, "k": s_ks, "r": s_rsig, "kv": s_fo}[kind]
            return s, 2 * step.job(stage) + n + 1

        def emptied(step, stage, kind, n):
            prev = step.tile_before(stage, kind, n)
            return released(prev[0], *prev[1]) if prev else (s_wl, WT)

        def steps(eng, body):
            for i in range(4):
                body(Step(0, i, i))
            with eng.Fori(0, (N - 6) // 2) as j:
                for u in range(2):
                    body(Step(j, 4 + u, 4))
            for i in range(N - 2, N + 2):
                body(Step(0, i, i))

        def next_a(st):
            i = 2 * st.j + st.c
            return 1 if isinstance(i, int) and i < 1 else 2 * i

        def tiles_w(name):
            _, k, m = wnames[name]
            return k * m // GT

        def w_tile(buf, t):
            return buf[:, t:t + 1, :] if buf.shape[2] == GT else buf[:, 2 * t:2 * t + 2, :]

        def w_bank(n, name):
            return ring[n % RING][:, :].rearrange("p (a b) -> p a b", b=wnames[name][2])

        WT = sum(tiles_w(n) for n in wnames)

        setup_w = list(wnames)

        def w_rows(n):
            return wnames[n][0].shape[0] // P

        block = ctx.enter_context(nc.Block())

        @block.sync
        def _(sp):
            sp.dma_start(xin[:, :, :], x_g[0]).then_inc(s_x, 16)
            sp.dma_start(gl[:, :], decay_log[None, :].to_broadcast((P, H))).then_inc(s_dmac, 16)
            for e in range(2):
                sp.dma_start(gpl[64 * e:64 * e + 64, :], decay_log.rearrange("(p e) -> e p", e=2)[e:e + 1, :].to_broadcast((64, PT)),
                             allow_slow_non_contiguous=True).then_inc(s_dmac, 16)
            sp.dma_start(bias[:, :], b_G[None, :].to_broadcast((P, HD))).then_inc(s_dmac, 16)
            sp.dma_start(mur[:, :], mu_r.rearrange("(k p) -> p k", p=P), allow_slow_non_contiguous=True).then_inc(s_dmac, 16)
            sp.dma_start(muk[:, :], mu_k.rearrange("(k p) -> p k", p=P), allow_slow_non_contiguous=True).then_inc(s_dmac, 16)
            for n, name in enumerate(setup_w):
                R, C = wnames[name][0].shape
                if n >= 2:
                    sp.wait_ge(s_wt, sum(tiles_w(z) for z in setup_w[:n - 1]))
                sp.dma_start(stage[n % 2][:, 0:R * C // P].rearrange("p (r c) -> p r c", c=C),
                             wnames[name][0].rearrange("(r p) c -> p r c", p=P)).then_inc(s_wload[n % 2], 16)

            def group(ap, g):
                return ap[g] if isinstance(g, int) else ap[bass.ds(g, 1)].rearrange("g p c d -> p (g c) d")

            def body(st):
                if st.has("A") and st.before < N - 1:
                    g, p, _ = st.g("A")
                    sp.wait_ge(s_res, 2 * (st.job("A") + 1))
                    sp.dma_start(xin[:, :, :], group(x_g, g + 1)).then_inc(s_x, 16)
                if st.has("C"):
                    g, p, _ = st.g("C")
                    sp.wait_ge(s_res, 2 * (st.job("C") + 1))
                    sp.dma_start(group(out_g, g), x2[p][:, :, :]).then_inc(s_out[p], 16)

            steps(sp, body)
            for p in range(2):
                sp.wait_ge(s_out[p], 16 * (N // 2))

        @block.gpsimd
        def _(pool):
            pool.memset(ident[:, :], 0.0).then_inc(s_const, 1)
            pool.memset(zeros[:, :], 0.0).then_inc(s_const, 1)
            pool.memset(m_half[:, :], -0.5)
            pool.memset(ln_eps[:, :], LN_EPS).then_inc(s_const, 1)
            for b in range(2):
                pool.memset(S[b][:, :, :], 0.0).then_inc(s_const, 1)
                pool.memset(kpad[b][:, :, :], 0.0).then_inc(s_const, 1)
            pool.memset(vv[:, :, :, DK:V1], 1.0).then_inc(s_const, 1)
            for s in "AC":
                pool.memset(xt[s][:, :, 0:1], 0.0).then_inc(s_const, 1)
            pool.wait_ge(s_const, 10)
            pool.affine_select(out=ident[:, :], in_=ident[:, :], compare_op=ALU.not_equal, fill=1.0,
                               base=0, pattern=[[-1, P]], channel_multiplier=1).then_inc(s_const, 1)

            def rstd(key, mv, rs, n):
                pool.wait_ge(s_var[key], n + 1)
                pool.tensor_tensor(rs[:, :], mv[:, :, 1], ln_eps[:, :], ALU.add).then_inc(s_rv[key], 1)
                pool.wait_ge(s_rv[key], n + 1)
                pool.tensor_tensor(rs[:, :], rs[:, :], m_half[:, :], ALU.pow).then_inc(s_rstd[key], 1)

            def shift_difference(st, s):
                J = st.job(s)
                _, p, _ = st.g(s)
                pool.wait_ge(s_xt, 2 * (J + 1))
                pool.wait_ge(s_ks, 2 * J)
                pool.tensor_tensor(dx[:, :, :], xt[s][:, :, 1:GT + 1], xt[s][:, :, 0:GT], ALU.subtract).then_inc(s_dx, 1)

            def decay_q(st, c):
                g, _, _ = st.g("B")
                pool.wait_ge(s_phi, 8 * g + 4)
                pool.wait_ge(s_num, 8 * g + 2 * c - 2 if c >= 2 else 8 * g)
                pool.tensor_tensor(qd[c % 2][:, :, :], qt[:, :, c * P:(c + 1) * P], qdec[:, :, :], ALU.mult).then_inc(s_qd, 1)

            def residual(st, s, t):
                J = st.job(s)
                g, p, h = st.g(s)
                src, dst = (xin, x1[p]) if s == "A" else (x2[p], x2[p])
                pool.wait_ge(s_fo, 2 * J + t + 1)
                if t == 0 and s == "A" and st.before >= 2:
                    pool.wait_ge(s_x2, 2 * (g - 1))
                pool.tensor_tensor(dst[:, 2 * t:2 * t + 2, :], src[:, 2 * t:2 * t + 2, :],
                                   fo[:, 2 * t:2 * t + 2, :], ALU.add).then_inc(s_res, 1)

            pool.wait_ge(s_const, 11)
            pool.wait_ge(s_setup, 1)
            rstd("f", mv_f, rs_f, 0)

            def body(st):
                a, b, c = st.has("A"), st.has("B"), st.has("C")
                if a:
                    shift_difference(st, "A")
                if c:
                    rstd("f", mv_f, rs_f, st.job("C"))
                if b:
                    decay_q(st, 0)
                    decay_q(st, 1)
                if c:
                    shift_difference(st, "C")
                if a:
                    for t in range(2):
                        residual(st, "A", t)
                if b:
                    decay_q(st, 2)
                if a:
                    rstd("b", mv_b, rs_b, st.g("A")[0])
                    if st.before < N - 1:
                        rstd("f", mv_f, rs_f, next_a(st))
                if b:
                    decay_q(st, 3)
                if c:
                    for t in range(2):
                        residual(st, "C", t)

            steps(pool, body)

        @block.scalar
        def _(act):
            act.wait_ge(s_dmac, 96)
            act.activation(gam[:, :], gl[:, :], ACT.Sigmoid).then_inc(s_gam, 1)
            act.activation(gamp[:, :], gpl[:, :], ACT.Sigmoid).then_inc(s_gam, 1)
            n = 0
            for name in setup_w:
                for t in range(tiles_w(name)):
                    act.wait_ge(s_wt, n + 1)
                    act.activation(w_tile(wh[name], t), w_bank(n, name), ACT.Copy).then_inc(s_wh, 1)
                    n += 1

            def x_high(st, k):
                g, _, _ = st.g("B")
                src = ring[st.tile("B", "xt", k)[0]]
                act.wait_ge(*filled(st, "B", "xt", k))
                act.wait_ge(s_gpre, 4 * g)
                act.activation(xth[:, k, :], src[:, :], ACT.Copy).then_inc(s_xth, 1)

            def x_turned(st, s, k):
                J = st.job(s)
                _, p, _ = st.g(s)
                src = ring[st.tile(s, "xt", k)[0]]
                act.wait_ge(*filled(st, s, "xt", k))
                act.wait_ge(s_mix["r"], KT * J)
                act.wait_ge(s_mix["k"], KT * J)
                if p == 0:
                    act.activation(xt[s][:, k, 0:1], zeros[:, 0:1], ACT.Copy).then_inc(s_carry, 1)
                else:
                    act.wait_ge(s_xt, 2 * J)
                    act.activation(xt[s][:, k, 0:1], xt[s][:, k, GT:GT + 1], ACT.Copy).then_inc(s_carry, 1)
                act.wait_ge(s_carry, 2 * J + k + 1)
                act.activation(xt[s][:, k, 1:GT + 1], src[:, :], ACT.Copy).then_inc(s_xt, 1)

            def exp(st, kind, d):
                g, _, _ = st.g("B")
                n = d + (4 if kind == "k" else 0)
                src = ring[st.tile("B", kind, d)[0]]
                act.wait_ge(*filled(st, "B", kind, d))
                if st.before > 1 or n > 1:
                    act.wait_ge(s_phi, 8 * g + n - 1)
                act.activation(ex[n % 2][:, :], src[:, :], ACT.Relu, scale=-1.0).then_inc(s_neg, 1)
                act.wait_ge(s_neg, 8 * g + n + 1)
                act.activation(ex[n % 2][:, :], ex[n % 2][:, :], ACT.Exp, scale=-1.0).then_inc(s_ex, 1)

            def mix_high(st, s, m):
                J = st.job(s)
                act.wait_ge(s_mix[m], KT * (J + 1))
                act.wait_ge(s_rsig if m == "r" else s_fo, 2 * J)
                act.activation(mixh[m][:, :, :], mix[m][:, :, :], ACT.Copy).then_inc(s_mixh[m], 1)

            def pad_k(st, d):
                g, _, _ = st.g("B")
                act.wait_ge(s_phi, 8 * g + 4 + d + 1)
                act.wait_ge(s_qk, 8 * g)
                act.activation(kpad[0][0:64, d, :], kt[0:64, d, :], ACT.Copy)
                act.activation(kpad[1][64:128, d, :], kt[64:128, d, :], ACT.Copy).then_inc(s_kpad, 1)

            def relu(st, s, d):
                J = st.job(s)
                src = ring[st.tile(s, "k", d)[0]]
                act.wait_ge(*filled(st, s, "k", d))
                act.wait_ge(s_mix["k"], KT * (J + 1))
                act.wait_ge(s_mix["r"], KT * (J + 1))
                act.activation(kr[:, d, :], src[:, :], ACT.Relu).then_inc(s_kr, 1)

            def square_high(st, s):
                J = st.job(s)
                act.wait_ge(s_ks, 2 * (J + 1))
                act.wait_ge(s_kr, 2 * (J + 1))
                act.activation(ksh[:, :, :], ks[:, :, :], ACT.Copy).then_inc(s_ksh, 1)

            def sigmoid_r(st, s, t):
                J = st.job(s)
                src = ring[st.tile(s, "r", t)[0]]
                act.wait_ge(*filled(st, s, "r", t))
                act.wait_ge(s_mixl["r"], J + 1)
                act.activation(rsig[:, 2 * t:2 * t + 2, :], src[:, :].rearrange("p (c d) -> p c d", c=2), ACT.Sigmoid).then_inc(s_rsig, 1)

            def values(st, c):
                g, _, _ = st.g("B")
                src = ring[st.tile("B", "v", c)[0]]
                act.wait_ge(*filled(st, "B", "v", c))
                act.wait_ge(s_num, 8 * g + 2 * c - 2 if c >= 1 else 8 * g)
                act.activation(vv[:, c % 2, :, 0:DK], src[:, :].rearrange("p (h e) -> p h e", h=H), ACT.Copy).then_inc(s_vv, 1)

            def sigmoid_gate(st, c):
                g, _, _ = st.g("B")
                act.wait_ge(s_gpre, 4 * g + c + 1)
                act.activation(gate[:, c % 2, :], gate[:, c % 2, :], ACT.Sigmoid).then_inc(s_gate, 1)

            def y_high(st, c):
                g, _, _ = st.g("B")
                src = ring[st.tile("B", "yt", c)[0]]
                act.wait_ge(*filled(st, "B", "yt", c))
                act.wait_ge(s_x2, 2 * g + c // 2)
                act.activation(yh[c % 2][:, :, :], src[:, :].rearrange("p (d t) -> p d t", t=P), ACT.Copy).then_inc(s_yh, 1)

            def body(st):
                a, b, c = st.has("A"), st.has("B"), st.has("C")
                if b:
                    x_high(st, 0)
                    x_high(st, 1)
                if a:
                    x_turned(st, "A", 0)
                    x_turned(st, "A", 1)
                if b:
                    exp(st, "q", 0)
                    exp(st, "q", 1)
                if a:
                    mix_high(st, "A", "k")
                if b:
                    exp(st, "q", 2)
                if a:
                    mix_high(st, "A", "r")
                if b:
                    exp(st, "q", 3)
                    for d in range(4):
                        exp(st, "k", d)
                        if d:
                            pad_k(st, d - 1)
                    pad_k(st, 3)
                if a:
                    relu(st, "A", 0)
                    relu(st, "A", 1)
                    square_high(st, "A")
                    sigmoid_r(st, "A", 0)
                    sigmoid_r(st, "A", 1)
                if b:
                    values(st, 0)
                    sigmoid_gate(st, 0)
                if c:
                    x_turned(st, "C", 0)
                    x_turned(st, "C", 1)
                if b:
                    values(st, 1)
                if c:
                    mix_high(st, "C", "k")
                    mix_high(st, "C", "r")
                if b:
                    sigmoid_gate(st, 1)
                if c:
                    relu(st, "C", 0)
                    relu(st, "C", 1)
                    square_high(st, "C")
                if b:
                    y_high(st, 0)
                    values(st, 2)
                    sigmoid_gate(st, 2)
                if c:
                    sigmoid_r(st, "C", 0)
                    sigmoid_r(st, "C", 1)
                if b:
                    y_high(st, 1)
                    values(st, 3)
                    sigmoid_gate(st, 3)
                    y_high(st, 2)
                    y_high(st, 3)

            steps(act, body)

        @block.vector
        def _(dve):
            n = 0
            for name in setup_w:
                for t in range(tiles_w(name)):
                    dve.wait_ge(s_wh, n + 1)
                    dve.tensor_tensor(w_tile(wl[name], t), w_bank(n, name), w_tile(wh[name], t).bitcast(F32), ALU.subtract).then_inc(s_wl, 1)
                    n += 1
            dve.wait_ge(s_gam, 2)
            dve.wait_ge(s_const, 11)
            for h in range(H):
                dve.tensor_tensor_scan(dmask[:, h, :], gam[:, h:h + 1].to_broadcast((P, P)), ident[:, :], 0.0, ALU.mult, ALU.add)
            for d in range(PT):
                last = dve.tensor_tensor_scan(qdec[:, d, :], gamp[:, d:d + 1].to_broadcast((P, P)), zeros[:, :], 1.0, ALU.mult, ALU.add)
            last.then_inc(s_setup, 1)
            dve.wait_ge(s_setup, 1)

            def ln_stats(key, src, st_, mv, n):
                for c in range(CH):
                    last = dve.bn_stats(st_[:, c, :], src[:, c, :])
                last.then_inc(s_stat[key], 1)
                dve.wait_ge(s_stat[key], n + 1)
                dve.memset(spare[:, :], 0.0)
                for c in range(CH):
                    last = dve.bn_aggr(mv[:, c, :], st_[:, c, :])
                last.then_inc(s_var[key], 1)

            def ln_scale(key, src, mv, rs, xn, n):
                dve.wait_ge(s_rstd[key], n + 1)
                for c in range(CH):
                    last = dve.tensor_scalar(xn[:, c, :], src[:, c, :], mv[:, c, 0:1], rs[:, c:c + 1], ALU.subtract, ALU.mult)
                last.then_inc(s_xn[key], 1)

            def stats_next_a(st):
                g, p, h = st.g("A", 1)
                dve.wait_ge(s_x, 16 * (g + 1))
                ln_stats("f", xin, st_f, mv_f, next_a(st))

            def scale_next_a(st):
                g, p, h = st.g("A", 1)
                n = next_a(st)
                dve.wait_ge(s_xt, 2 * n)
                ln_scale("f", xin, mv_f, rs_f, xn_f, n)

            def stats_c(st):
                g, p, h = st.g("C")
                dve.wait_ge(s_x2, 2 * (g + 1))
                ln_stats("f", x2[p], st_f, mv_f, st.job("C"))

            def scale_c(st):
                g, p, h = st.g("C")
                dve.wait_ge(s_xt, 2 * st.job("C"))
                ln_scale("f", x2[p], mv_f, rs_f, xn_f, st.job("C"))

            def stats_b(st):
                g, p, h = st.g("A")
                dve.wait_ge(s_res, 2 * (st.job("A") + 1))
                ln_stats("b", x1[p], st_b, mv_b, g)

            def scale_b(st):
                g, p, h = st.g("A")
                dve.wait_ge(s_xth, 2 * g)
                ln_scale("b", x1[p], mv_b, rs_b, xn_b, g)

            def x_low(st, k):
                g, _, _ = st.g("B")
                src = ring[st.tile("B", "xt", k)[0]]
                dve.wait_ge(*filled(st, "B", "xt", k))
                dve.wait_ge(s_xth, 2 * g + k + 1)
                dve.tensor_tensor(xtl[:, k, :], src[:, :], xth[:, k, :].bitcast(F32), ALU.subtract).then_inc(s_xtl, 1)

            def mixes(st, s, m):
                J = st.job(s)
                _, p, _ = st.g(s)
                mu = muk if m == "k" else mur
                dve.wait_ge(s_dx, J + 1)
                if m == "k":
                    dve.wait_ge(s_ksh, J)
                    dve.wait_ge(s_ksl, J)
                else:
                    dve.wait_ge(s_res, 2 * J)
                for k in range(KT):
                    dve.scalar_tensor_tensor(mix[m][:, k, :], dx[:, k, :], mu[:, k:k + 1], xt[s][:, k, 0:GT],
                                             ALU.mult, ALU.add).then_inc(s_mix[m], 1)

            def mix_low(st, s, m):
                J = st.job(s)
                dve.wait_ge(s_mixh[m], J + 1)
                dve.tensor_tensor(mixl[m][:, :, :], mix[m][:, :, :], mixh[m][:, :, :].bitcast(F32), ALU.subtract).then_inc(s_mixl[m], 1)

            def phi(st, kind, d):
                g, _, _ = st.g("B")
                n = d + (4 if kind == "k" else 0)
                src = ring[st.tile("B", kind, d)[0]]
                dve.wait_ge(*filled(st, "B", kind, d))
                dve.wait_ge(s_ex, 8 * g + n + 1)
                if n == 0:
                    dve.wait_ge(s_qk, 8 * g)
                    dve.wait_ge(s_qd, 4 * g)
                if n == 4:
                    dve.wait_ge(s_kpad, 4 * g)
                    dve.wait_ge(s_kd, 4 * g)
                dst = qt if kind == "q" else kt
                dve.scalar_tensor_tensor(dst[:, d, :], src[:, :], 1.0, ex[n % 2][:, :], ALU.add, ALU.max).then_inc(s_phi, 1)

            def square(st, s, d):
                J = st.job(s)
                src = ring[st.tile(s, "k", d)[0]]
                dve.wait_ge(*filled(st, s, "k", d))
                dve.wait_ge(s_kr, 2 * J + d + 1)
                dve.wait_ge(s_mixh["k"], J + 1)
                dve.wait_ge(s_mixl["k"], J + 1)
                dve.tensor_tensor(ks[:, d, :], src[:, :], kr[:, d, :], ALU.mult).then_inc(s_ks, 1)

            def square_low(st, s):
                J = st.job(s)
                dve.wait_ge(s_ksh, J + 1)
                dve.tensor_tensor(ksl[:, :, :], ks[:, :, :], ksh[:, :, :].bitcast(F32), ALU.subtract).then_inc(s_ksl, 1)

            def decay_k(st, c):
                g, _, _ = st.g("B")
                src = ring[st.tile("B", "kt", c)[0]]
                dve.wait_ge(*filled(st, "B", "kt", c))
                if c >= 2:
                    dve.wait_ge(s_S, 8 * g + 2 * c - 2)
                dve.tensor_tensor(kd[c % 2][:, :].rearrange("p (h e) -> p h e", h=H),
                                  src[:, :].rearrange("p (h e) -> p h e", h=H),
                                  dmask[:, :, P - 1:P].to_broadcast((P, H, DK)), ALU.mult).then_inc(s_kd, 1)

            def mask_scores(st, c):
                g, _, _ = st.g("B")
                for half in range(2):
                    dve.wait_ge(s_qk, 8 * g + 2 * c + half + 1)
                    if half == 0 and c >= 2:
                        dve.wait_ge(s_num, 8 * g + 2 * c - 2)
                    dve.tensor_tensor(at[c % 2][:, 4 * half:4 * half + 4, :], ps_qk[half][:, :, :],
                                      dmask[:, 4 * half:4 * half + 4, :], ALU.mult).then_inc(s_at, 1)

            def gate_bias(st, c):
                g, _, _ = st.g("B")
                src = ring[st.tile("B", "g", c)[0]]
                dve.wait_ge(*filled(st, "B", "g", c))
                dve.wait_ge(s_y, 8 * g + 2 * c - 2 if c >= 2 else 8 * g)
                dve.tensor_tensor(gate[:, c % 2, :], src[:, :], bias[:, :], ALU.add).then_inc(s_gpre, 1)

            def state(st, c):
                g, p, _ = st.g("B")
                dve.wait_ge(s_num, 8 * g + 2 * c)
                for r in range(2):
                    src = ring[st.tile("B", "s", 2 * c + r)[0]]
                    dve.wait_ge(*filled(st, "B", "s", 2 * c + r))
                    dve.wait_ge(s_S, 8 * g + 2 * c)
                    for d in (2 * r, 2 * r + 1):
                        for e in range(2):
                            rows, cols = slice(64 * e, 64 * e + 64), slice(V1 * e, V1 * e + V1)
                            at_ps = 2 * V1 * (d - 2 * r) + V1 * e
                            new, got = S[(c + 1) % 2][rows, d, cols], src[rows, at_ps:at_ps + V1]
                            if p == 0 and c == 0:
                                last = dve.tensor_copy(new, got)
                            else:
                                last = dve.scalar_tensor_tensor(new, S[c % 2][rows, d, cols], qdec[rows, d, P - 1:P], got,
                                                                ALU.mult, ALU.add)
                    last.then_inc(s_S, 1)

            def outputs(st, c):
                g, _, _ = st.g("B")
                for half in range(2):
                    dve.wait_ge(s_num, 8 * g + 2 * c + half + 1)
                    num = ps_num[half][:, 0:4 * V1].rearrange("p (h e) -> p h e", e=V1)
                    dve.tensor_scalar(den[:, 4 * half:4 * half + 4], num[:, :, DK], DEN_EPS, None, ALU.add).then_inc(s_den, 1)
                    dve.wait_ge(s_den, 8 * g + 2 * c + half + 1)
                    dve.reciprocal(rden[:, 4 * half:4 * half + 4], den[:, 4 * half:4 * half + 4]).then_inc(s_rden, 1)
                    dve.wait_ge(s_rden, 8 * g + 2 * c + half + 1)
                    dve.wait_ge(s_gate, 4 * g + c + 1)
                    dve.wait_ge(s_yl, 4 * g + c)
                    for h in range(4 * half, 4 * half + 4):
                        last = dve.scalar_tensor_tensor(y[:, h * DK:(h + 1) * DK], num[:, h % 4, 0:DK], rden[:, h:h + 1],
                                                        gate[:, c % 2, h * DK:(h + 1) * DK], ALU.mult, ALU.mult)
                    last.then_inc(s_y, 1)

            def y_low(st, c):
                g, _, _ = st.g("B")
                src = ring[st.tile("B", "yt", c)[0]]
                dve.wait_ge(*filled(st, "B", "yt", c))
                dve.wait_ge(s_yh, 4 * g + c + 1)
                dve.wait_ge(s_x2, 2 * g + c // 2)
                dve.tensor_tensor(yl[c % 2][:, :, :], src[:, :].rearrange("p (d t) -> p d t", t=P),
                                  yh[c % 2][:, :, :].bitcast(F32), ALU.subtract).then_inc(s_yl, 1)

            def residual_b(st, t):
                g, p, h = st.g("B")
                src = ring[st.tile("B", "o", t)[0]]
                dve.wait_ge(*filled(st, "B", "o", t))
                dve.wait_ge(s_out[p], 16 * h)
                dve.tensor_tensor(x2[p][:, 2 * t:2 * t + 2, :], src[:, :].rearrange("p (c d) -> p c d", c=2),
                                  x1[p][:, 2 * t:2 * t + 2, :], ALU.add).then_inc(s_x2, 1)

            def gated(st, s, t):
                J = st.job(s)
                src = ring[st.tile(s, "kv", t)[0]]
                dve.wait_ge(*filled(st, s, "kv", t))
                dve.wait_ge(s_rsig, 2 * J + t + 1)
                dve.scalar_tensor_tensor(fo[:, 2 * t:2 * t + 2, :], src[:, :].rearrange("p (c d) -> p c d", c=2), 0.5,
                                         rsig[:, 2 * t:2 * t + 2, :], ALU.mult, ALU.mult).then_inc(s_fo, 1)

            dve.wait_ge(s_x, 16)
            ln_stats("f", xin, st_f, mv_f, 0)
            ln_scale("f", xin, mv_f, rs_f, xn_f, 0)
            dve.wait_ge(s_dmac, 96)

            def body(st):
                a, b, c = st.has("A"), st.has("B"), st.has("C")
                more = st.before < N - 1
                if b:
                    x_low(st, 0)
                    x_low(st, 1)
                    phi(st, "q", 0)
                if a:
                    mixes(st, "A", "k")
                if b:
                    phi(st, "q", 1)
                if a:
                    mixes(st, "A", "r")
                if b:
                    phi(st, "q", 2)
                if a:
                    mix_low(st, "A", "k")
                if b:
                    phi(st, "q", 3)
                if a:
                    mix_low(st, "A", "r")
                if b:
                    phi(st, "k", 0)
                    phi(st, "k", 1)
                if c:
                    stats_c(st)
                if b:
                    phi(st, "k", 2)
                    phi(st, "k", 3)
                if c:
                    scale_c(st)
                if a:
                    square(st, "A", 0)
                    square(st, "A", 1)
                    square_low(st, "A")
                if b:
                    decay_k(st, 0)
                    mask_scores(st, 0)
                    gate_bias(st, 0)
                if a:
                    gated(st, "A", 0)
                    gated(st, "A", 1)
                if c:
                    mixes(st, "C", "k")
                    mixes(st, "C", "r")
                if b:
                    decay_k(st, 1)
                    mask_scores(st, 1)
                if c:
                    mix_low(st, "C", "k")
                    mix_low(st, "C", "r")
                if b:
                    gate_bias(st, 1)
                    state(st, 0)
                    outputs(st, 0)
                if c:
                    square(st, "C", 0)
                    square(st, "C", 1)
                    square_low(st, "C")
                if b:
                    y_low(st, 0)
                    decay_k(st, 2)
                    mask_scores(st, 2)
                    gate_bias(st, 2)
                    state(st, 1)
                    outputs(st, 1)
                if a:
                    stats_b(st)
                if b:
                    y_low(st, 1)
                    residual_b(st, 0)
                    decay_k(st, 3)
                    mask_scores(st, 3)
                    gate_bias(st, 3)
                if a:
                    scale_b(st)
                if a and more:
                    stats_next_a(st)
                if b:
                    state(st, 2)
                    outputs(st, 2)
                    y_low(st, 2)
                if a and more:
                    scale_next_a(st)
                if b:
                    state(st, 3)
                    outputs(st, 3)
                if c:
                    gated(st, "C", 0)
                    gated(st, "C", 1)
                if b:
                    y_low(st, 3)
                    residual_b(st, 1)

            steps(dve, body)

        @block.tensor
        def _(pe):
            pe.wait_ge(s_const, 11)
            n = 0
            for w, name in enumerate(setup_w):
                pe.wait_ge(s_wload[w % 2], 16 * (w // 2 + 1))
                W, k, m = wnames[name]
                C = W.shape[1]
                for t in range(tiles_w(name)):
                    if n >= RING:
                        pe.wait_ge(s_wl, n - RING + 1)
                    for z in range(4):
                        kk, r = (t, z) if m == GT else (2 * t + z // 2, z % 2)
                        last = pe.transpose(ring[n % RING][:, z * P:(z + 1) * P], stage[w % 2][:, r * C + kk * P:r * C + (kk + 1) * P], ident[:, :])
                    last.then_inc(s_wt, 1)
                    n += 1
            pe.wait_ge(s_wl, WT)

            def three_passes(out, lhs, rhs, first=True, last=True):
                (lh, ll), (rh, rl) = lhs, rhs
                pe.matmul(out, ll, rh, start=first, stop=False)
                pe.matmul(out, lh, rl, start=False, stop=False)
                return pe.matmul(out, lh, rh, start=False, stop=last)

            def turn(st, s, k):
                xn, key = (xn_b, "b") if s == "B" else (xn_f, "f")
                n = st.g("B")[0] if s == "B" else st.job(s)
                pe.wait_ge(s_xn[key], n + 1)
                pe.wait_ge(*emptied(st, s, "xt", k))
                b, _ = st.tile(s, "xt", k)
                for c in range(CH):
                    last = pe.transpose(ring[b][:, c * P:(c + 1) * P], xn[:, c, k * P:(k + 1) * P], ident[:, :])
                last.then_inc(ready[b], 1)

            def project(st, kind, d):
                g, _, _ = st.g("B")
                pe.wait_ge(s_xtl, 2 * (g + 1))
                pe.wait_ge(*emptied(st, "B", kind, d))
                b, _ = st.tile("B", kind, d)
                cols = slice(d * P, (d + 1) * P)
                for k in range(KT):
                    last = three_passes(ring[b][:, :], (wh[kind][:, k, cols], wl[kind][:, k, cols]),
                                        (xth[:, k, :], xtl[:, k, :]), k == 0, k == KT - 1)
                last.then_inc(ready[b], 1)

            def project_tokens(st, kind, c):
                pe.wait_ge(*emptied(st, "B", kind, c))
                b, _ = st.tile("B", kind, c)
                cols = slice(c * P, (c + 1) * P)
                for k in range(KT):
                    last = three_passes(ring[b][:, :], (xth[:, k, cols], xtl[:, k, cols]),
                                        (wh[kind][:, k, :], wl[kind][:, k, :]), k == 0, k == KT - 1)
                last.then_inc(ready[b], 1)

            def turn_k(st, c):
                g, _, _ = st.g("B")
                pe.wait_ge(s_phi, 8 * (g + 1))
                pe.wait_ge(*emptied(st, "B", "kt", c))
                b, _ = st.tile("B", "kt", c)
                for d in range(PT):
                    last = pe.transpose(ring[b][:, d * P:(d + 1) * P], kt[:, d, c * P:(c + 1) * P], ident[:, :])
                last.then_inc(ready[b], 1)

            def scores(st, c):
                g, _, _ = st.g("B")
                pe.wait_ge(s_kpad, 4 * (g + 1))
                for half in range(2):
                    pe.wait_ge(s_at, 8 * g + 2 * c + half - 1 if c + half else 8 * g)
                    for h in range(4):
                        d = 2 * half + h // 2
                        last = pe.matmul(ps_qk[half][:, h, :], kpad[h % 2][:, d, c * P:(c + 1) * P],
                                         qt[:, d, c * P:(c + 1) * P], start=True, stop=True)
                    last.then_inc(s_qk, 1)

            def state_products(st, c, r):
                g, _, _ = st.g("B")
                pe.wait_ge(s_kd, 4 * g + c + 1)
                pe.wait_ge(s_vv, 4 * g + c + 1)
                pe.wait_ge(*emptied(st, "B", "s", 2 * c + r))
                b, _ = st.tile("B", "s", 2 * c + r)
                for d in (2 * r, 2 * r + 1):
                    last = pe.matmul(ring[b][:, 2 * V1 * (d - 2 * r):2 * V1 * (d - 2 * r + 1)], kd[c % 2][:, d * P:(d + 1) * P],
                                     vv[:, c % 2, 2 * d:2 * d + 2, :].rearrange("p h e -> p (h e)"), start=True, stop=True)
                last.then_inc(ready[b], 1)

            def numerators(st, c):
                g, p, _ = st.g("B")
                fresh = p == 0 and c == 0
                pe.wait_ge(s_vv, 4 * g + c + 1)
                for half in range(2):
                    pe.wait_ge(s_at, 8 * g + 2 * c + half + 1)
                    pe.wait_ge(s_y, 8 * g + 2 * c + half - 1 if c + half else 8 * g)
                    pe.wait_ge(s_qd, 4 * g + c + 1)
                    if not fresh:
                        pe.wait_ge(s_S, 8 * g + 2 * c)
                    for dd in range(2):
                        d = 2 * half + dd
                        at_ps = 2 * V1 * dd
                        if not fresh:
                            pe.matmul(ps_num[half][:, at_ps:at_ps + 2 * V1], qd[c % 2][:, d, :], S[c % 2][:, d, :],
                                      start=True, stop=False)
                        for e in range(2):
                            last = pe.matmul(ps_num[half][:, at_ps + V1 * e:at_ps + V1 * e + V1], at[c % 2][:, 2 * d + e, :],
                                             vv[:, c % 2, 2 * d + e, :], start=fresh, stop=fresh or e == 1)
                    last.then_inc(s_num, 1)

            def turn_y(st, c):
                g, _, _ = st.g("B")
                pe.wait_ge(s_y, 8 * g + 2 * c + 2)
                pe.wait_ge(*emptied(st, "B", "yt", c))
                b, _ = st.tile("B", "yt", c)
                for d in range(PT):
                    last = pe.transpose(ring[b][:, d * P:(d + 1) * P], y[:, d * P:(d + 1) * P], ident[:, :])
                last.then_inc(ready[b], 1)

            def project_out(st, t):
                g, _, _ = st.g("B")
                pe.wait_ge(s_yl, 4 * g + 2 * t + 2)
                pe.wait_ge(*emptied(st, "B", "o", t))
                b, _ = st.tile("B", "o", t)
                for z in range(2):
                    for d in range(PT):
                        last = three_passes(ring[b][:, z * D:(z + 1) * D], (yh[z][:, d, :], yl[z][:, d, :]),
                                            (wh["o"][:, d, :], wl["o"][:, d, :]), d == 0, d == PT - 1)
                last.then_inc(ready[b], 1)

            def ffn_k(st, s, d):
                J = st.job(s)
                pe.wait_ge(s_mixl["k"], J + 1)
                pe.wait_ge(*emptied(st, s, "k", d))
                b, _ = st.tile(s, "k", d)
                cols = slice(d * P, (d + 1) * P)
                for k in range(KT):
                    last = three_passes(ring[b][:, :], (wh["fk"][:, k, cols], wl["fk"][:, k, cols]),
                                        (mixh["k"][:, k, :], mixl["k"][:, k, :]), k == 0, k == KT - 1)
                last.then_inc(ready[b], 1)

            def ffn_tokens(st, s, kind, t):
                J = st.job(s)
                if kind == "r":
                    pe.wait_ge(s_mixl["r"], J + 1)
                    xh_, xl_, w = mixh["r"], mixl["r"], "fr"
                else:
                    pe.wait_ge(s_ksl, J + 1)
                    xh_, xl_, w = ksh, ksl, "fv"
                pe.wait_ge(*emptied(st, s, kind, t))
                b, _ = st.tile(s, kind, t)
                for z in range(2):
                    cols = slice((2 * t + z) * P, (2 * t + z + 1) * P)
                    for k in range(KT):
                        last = three_passes(ring[b][:, z * D:(z + 1) * D], (xh_[:, k, cols], xl_[:, k, cols]),
                                            (wh[w][:, k, :], wl[w][:, k, :]), k == 0, k == KT - 1)
                last.then_inc(ready[b], 1)

            def body(st):
                a, b, c = st.has("A"), st.has("B"), st.has("C")
                if b:
                    turn(st, "B", 0)
                    turn(st, "B", 1)
                if a:
                    turn(st, "A", 0)
                    turn(st, "A", 1)
                if b:
                    project(st, "q", 0)
                    project(st, "q", 1)
                    project(st, "q", 2)
                    project(st, "q", 3)
                    project(st, "k", 0)
                    project(st, "k", 1)
                    project(st, "k", 2)
                    project(st, "k", 3)
                if a:
                    ffn_k(st, "A", 0)
                    ffn_k(st, "A", 1)
                    ffn_tokens(st, "A", "r", 0)
                    ffn_tokens(st, "A", "r", 1)
                if b:
                    project_tokens(st, "v", 0)
                    turn_k(st, 0)
                    scores(st, 0)
                    project_tokens(st, "g", 0)
                if c:
                    turn(st, "C", 0)
                    turn(st, "C", 1)
                if b:
                    project_tokens(st, "v", 1)
                if a:
                    ffn_tokens(st, "A", "kv", 0)
                    ffn_tokens(st, "A", "kv", 1)
                if b:
                    turn_k(st, 1)
                    scores(st, 1)
                    project_tokens(st, "g", 1)
                    state_products(st, 0, 0)
                    state_products(st, 0, 1)
                    numerators(st, 0)
                if c:
                    ffn_k(st, "C", 0)
                    ffn_k(st, "C", 1)
                if b:
                    turn_y(st, 0)
                    project_tokens(st, "v", 2)
                    turn_k(st, 2)
                    scores(st, 2)
                    project_tokens(st, "g", 2)
                    state_products(st, 1, 0)
                    state_products(st, 1, 1)
                    numerators(st, 1)
                if c:
                    ffn_tokens(st, "C", "r", 0)
                    ffn_tokens(st, "C", "r", 1)
                if b:
                    turn_y(st, 1)
                    project_tokens(st, "v", 3)
                    project_out(st, 0)
                    turn_k(st, 3)
                    scores(st, 3)
                    project_tokens(st, "g", 3)
                    state_products(st, 2, 0)
                    state_products(st, 2, 1)
                    numerators(st, 2)
                    turn_y(st, 2)
                    state_products(st, 3, 0)
                    state_products(st, 3, 1)
                    numerators(st, 3)
                if c:
                    ffn_tokens(st, "C", "kv", 0)
                    ffn_tokens(st, "C", "kv", 1)
                if b:
                    turn_y(st, 3)
                    project_out(st, 1)

            steps(pe, body)


_INS = ["x", "W_Q", "W_K", "W_V", "W_g_w", "W_g_b", "W_O", "decay_log"]
_FFN = ["W_r", "W_k", "W_v", "mu_r", "mu_k"]


def kernel(**inputs):
    import numpy as _np
    import concourse.bacc as _bacc
    from concourse import mybir as _mybir
    from concourse.bass_utils import run_bass_kernel_spmd as _run

    nc = _bacc.Bacc("TRN2", target_bir_lowering=False, num_devices=1)
    arrays, args = {}, []
    for name in ["L0_attn_" + n for n in _INS] + ["L0_ffn_" + n for n in _FFN]:
        a = _np.ascontiguousarray(inputs[name])
        arrays[f"in_{name}_dram"] = a
        args.append(nc.dram_tensor(f"in_{name}_dram", a.shape, _mybir.dt.from_np(a.dtype), kind="ExternalInput").ap())
    shape = inputs["L0_attn_x"].shape
    args.append(nc.dram_tensor("out_0_dram", shape, _mybir.dt.float32, kind="ExternalOutput").ap())
    macaron(nc, *args)
    r = _run(nc, [arrays], core_ids=[0])
    return r.results[0]["out_0_dram"]
```

```python
from contextlib import ExitStack

import concourse.bass as bass
from concourse import mybir

F32 = mybir.dt.float32
F32R = mybir.dt.float32r
ACT = mybir.ActivationFunctionType
ALU = mybir.AluOpType

P = 128
CH = 4
GT = CH * P
RING = 4
LN_EPS = 1e-5
DEN_EPS = 1e-6

OFF_RING = ("qk", "num")
ORDER = (
    "Bxt0 Bxt1 Axt0 Axt1 Bq0 Bq1 Bg0 Bq2 Bq3 Bk0 Bg1 Bk1 Ak0 Bk2 Bk3 Ak1 Ar0 Ar1 Bv0 Akv0 Akv1 Bv1 "
    "Cxt0 Cxt1 Bqk0 Bkt0 Bkt1 Bnum0 Bs0 Bg2 Bs1 Bqk1 Bv2 Bs2 Byt0 Bs3 Bnum1 Bqk2 Bg3 Ck0 Ck1 Byt1 "
    "Bnum2 Bkt2 Bo0 Bs4 Bqk3 Bv3 Bs5 Cr0 Byt2 Bnum3 Bkt3 Cr1 Byt3 Ckv0 Bs6 Ckv1 Bs7 Bo1 "
).split()
LAG = {"A": 0, "B": 1, "C": 2}


def tiles_of(stages):
    return [t for t in ((w[0], w[1:-1], int(w[-1])) for w in ORDER) if t[0] in stages and t[1] not in OFF_RING]


def macaron(nc, x, W_Q, W_K, W_V, W_G, b_G, W_O, decay_log, W_r, W_k, W_v, mu_r, mu_k, out):
    B, T, D = x.shape
    HD = W_Q.shape[0]
    H = decay_log.shape[0]
    DK = HD // H
    KT = D // P
    PT = HD // P
    V1 = DK + 1
    N = B * T // GT
    assert T == 2 * GT and D == 2 * P and HD == 4 * P and DK == 64 and H == 8

    stages_at = [[s for s in "ABC" if 0 <= i - LAG[s] < N] for i in range(N + 2)]
    full = len(tiles_of("ABC"))
    assert full % RING == 0 and all(sum(len(tiles_of(s)) for s in stages_at[:i]) % RING == 0 for i in range(5))

    x_g = x.rearrange("b (g c p) d -> (b g) p c d", c=CH, p=P)
    out_g = out.rearrange("b (g c p) d -> (b g) p c d", c=CH, p=P)

    with ExitStack() as ctx:
        def sb(name, shape, dt=F32):
            return ctx.enter_context(nc.sbuf_tensor(name, shape, dt))

        def sem(name):
            return ctx.enter_context(nc.semaphore(name))

        ring = [ctx.enter_context(nc.psum_tensor(f"ring{b}", [P, GT], F32)) for b in range(RING)]
        ps_qk = [ctx.enter_context(nc.psum_tensor(f"ps_qk{b}", [P, 4, P], F32)) for b in range(2)]
        ps_num = [ctx.enter_context(nc.psum_tensor(f"ps_num{b}", [P, 512], F32)) for b in range(2)]

        ident = sb("ident", [P, P])
        zero = sb("zero", [P, 1])
        m_half = sb("m_half", [P, CH])
        ln_eps = sb("ln_eps", [P, CH])
        m_one = sb("m_one", [P, CH])
        spare = sb("spare", [P, 1])
        gl = sb("gl", [P, H])
        gpl = sb("gpl", [P, PT])
        gam = sb("gam", [P, H])
        gamp = sb("gamp", [P, PT])
        dmask = sb("dmask", [P, H, P])
        power = sb("power", [P, PT, P + 1])
        qdec = power[:, :, 1:P + 1]
        kdec = power[:, :, P - 1::-1]
        bias = sb("bias", [P, HD])
        mur = sb("mur", [P, KT])
        muk = sb("muk", [P, KT])
        wnames = {"q": (W_Q, KT, HD), "k": (W_K, KT, HD), "v": (W_V, KT, HD), "g": (W_G, KT, HD),
                  "o": (W_O, PT, D), "fr": (W_r, KT, D), "fk": (W_k, KT, D), "fv": (W_v, KT, D)}
        wh = {n: sb(f"wh_{n}", [P, k, m], F32R) for n, (_, k, m) in wnames.items()}
        wl = {n: sb(f"wl_{n}", [P, k, m], F32R) for n, (_, k, m) in wnames.items()}

        xin = sb("xin", [P, CH, D])
        x1 = [sb(f"x1_{p}", [P, CH, D]) for p in range(2)]
        x2 = [sb(f"x2_{p}", [P, CH, D]) for p in range(2)]

        st_f, mv_f, rs_f, nm_f, xn_f = sb("st_f", [P, CH, 6]), sb("mv_f", [P, CH, 2]), sb("rs_f", [P, CH]), sb("nm_f", [P, CH]), sb("xn_f", [P, CH, D])
        xt = sb("xt", [P, KT, 1 + GT])
        carry = {s: sb(f"carry_{s}", [P, KT, 1]) for s in "AC"}
        dx = sb("dx", [P, KT, GT])
        mix = {m: sb(f"mix_{m}", [P, KT, GT]) for m in "kr"}
        mixh = {m: sb(f"mixh_{m}", [P, KT, GT], F32R) for m in "kr"}
        mixl = {m: sb(f"mixl_{m}", [P, KT, GT], F32R) for m in "kr"}
        kr, ks, ksh, ksl = dx, mix["k"], mixh["k"], mixl["k"]
        rsig = fo = mix["r"][:, :, :].rearrange("p k (c d) -> p (k c) d", d=D)

        st_b, mv_b, rs_b, nm_b = sb("st_b", [P, CH, 6]), sb("mv_b", [P, CH, 2]), sb("rs_b", [P, CH]), sb("nm_b", [P, CH])
        xn_b = dx[:, :, :].rearrange("p k (c d) -> p (k c) d", d=D)
        xth = sb("xth", [P, KT, GT], F32R)
        xtl = sb("xtl", [P, KT, GT], F32R)
        ex = [sb(f"ex{b}", [P, GT]) for b in range(2)]
        qt = sb("qt", [P, PT, GT])
        qd = [sb(f"qd{b}", [P, PT, P]) for b in range(2)]
        kt = sb("kt", [P, PT, GT])
        kh, kl = sb("kh", [P, PT, GT], F32R), sb("kl", [P, PT, GT], F32R)
        qh, ql = sb("qh", [P, PT, 2, P], F32R), sb("ql", [P, PT, 2, P], F32R)
        vv = sb("vv", [P, 2, H, V1])
        gate = sb("gate", [P, 2, HD])
        kd = [sb(f"kd{b}", [P, HD]) for b in range(2)]
        at = [sb(f"at{b}", [P, H, P]) for b in range(2)]
        S = [sb(f"S{b}", [P, PT, 2 * V1]) for b in range(2)]
        den = sb("den", [P, H])
        rden = sb("rden", [P, H])
        y = sb("y", [P, HD])
        yh = [sb(f"yh{b}", [P, PT, P], F32R) for b in range(2)]
        yl = [sb(f"yl{b}", [P, PT, P], F32R) for b in range(2)]

        s_ident = sem("s_ident")
        s_const, s_setup = sem("s_const"), sem("s_setup")
        s_mu, s_decay, s_bias = sem("s_mu"), sem("s_decay"), sem("s_bias")
        s_wload = {n: sem(f"s_wload_{n}") for n in wnames}
        s_wt, s_wh, s_wl = sem("s_wt"), sem("s_wh"), sem("s_wl")
        s_kdec = sem("s_kdec")
        s_gam, s_carry, s_neg = sem("s_gam"), sem("s_carry"), sem("s_neg")
        s_x = sem("s_x")
        s_out = [sem(f"s_out{p}") for p in range(2)]
        ready = [sem(f"ring_ready{b}") for b in range(RING)]
        s_stat, s_var, s_rv, s_rstd, s_xn = [{k: sem(f"s_{n}_{k}") for k in "fb"} for n in ("stat", "var", "rv", "rstd", "xn")]
        s_xt, s_dx, s_mix = sem("s_xt"), sem("s_dx"), {m: sem(f"s_mix_{m}") for m in "kr"}
        s_mixh, s_mixl = {m: sem(f"s_mixh_{m}") for m in "kr"}, {m: sem(f"s_mixl_{m}") for m in "kr"}
        s_kr, s_ks, s_ksh, s_ksl, s_rsig, s_fo, s_res = [sem("s_" + n) for n in ("kr", "ks", "ksh", "ksl", "rsig", "fo", "res")]
        s_xth, s_xtl, s_ex, s_phi, s_kh, s_kl, s_qh, s_ql, s_qd = [sem("s_" + n) for n in ("xth", "xtl", "ex", "phi", "kh", "kl", "qh", "ql", "qd")]
        s_vv, s_gpre, s_gate, s_kd, s_qk, s_at = [sem("s_" + n) for n in ("vv", "gpre", "gate", "kd", "qk", "at")]
        s_S, s_num, s_den, s_rden, s_y, s_yh, s_yl, s_x2 = [sem("s_" + n) for n in ("S", "num", "den", "rden", "y", "yh", "yl", "x2")]

        class Step:

            def __init__(self, j, c, typical):
                self.j, self.c = j, c
                self.stages = stages_at[typical]
                self.before = typical

            def g(self, stage, ahead=0):
                k = self.c + ahead - LAG[stage]
                return 2 * self.j + k, k % 2, self.j + k // 2

            def job(self, stage):
                i = 2 * self.j + self.c
                if isinstance(i, int) and i < 2:
                    return i
                if isinstance(i, int) and i >= N:
                    return 2 * N - 2 + i - N
                return 2 * i - (2 if stage == "A" else 1)

            def tile(self, stage, kind, n):
                done = sum(len(tiles_of(s)) for s in stages_at[:self.c])
                at = done + tiles_of(self.stages).index((stage, kind, n))
                return at % RING, 2 * (full // RING) * self.j + at // RING + 1

            def tile_before(self, stage, kind, n):
                at = tiles_of(self.stages).index((stage, kind, n)) - RING
                if at >= 0:
                    return self, tiles_of(self.stages)[at]
                if self.c == 0:
                    return None
                last = Step(self.j, self.c - 1, self.before - 1 if isinstance(self.j, int) else self.before)
                return last, tiles_of(last.stages)[at]

            def has(self, stage):
                return stage in self.stages

        def filled(step, stage, kind, n):
            b, count = step.tile(stage, kind, n)
            return ready[b], count

        def released(step, stage, kind, n):
            if stage == "B":
                g, _, _ = step.g("B")
                s, per = {"xt": (s_xtl, 2), "q": (s_phi, 8), "k": (s_phi, 8), "v": (s_vv, 4), "g": (s_gpre, 4),
                          "kt": (s_kd, 4), "s": (s_S, 8), "yt": (s_yl, 4), "o": (s_x2, 2)}[kind]
                return s, per * g + n + 1 + (4 if kind == "k" else 0)
            s = {"xt": s_xt, "k": s_ks, "r": s_rsig, "kv": s_fo}[kind]
            return s, 2 * step.job(stage) + n + 1

        def emptied(step, stage, kind, n):
            prev = step.tile_before(stage, kind, n)
            return released(prev[0], *prev[1]) if prev else (s_ident, 2)

        def steps(eng, body):
            for i in range(4):
                body(Step(0, i, i))
            with eng.Fori(0, (N - 6) // 2) as j:
                for u in range(2):
                    body(Step(j, 4 + u, 4))
            for i in range(N - 2, N + 2):
                body(Step(0, i, i))

        def next_a(st):
            i = 2 * st.j + st.c
            return 1 if isinstance(i, int) and i < 1 else 2 * i

        def tiles_w(name):
            _, k, m = wnames[name]
            return k * m // GT

        def w_tile(buf, t):
            return buf[:, t:t + 1, :] if buf.shape[2] == GT else buf[:, 2 * t:2 * t + 2, :]

        setup_w = ["fk", "fr", "fv", "q", "k", "v", "g", "o"]
        w_tiles = [(n, t) for n in setup_w for t in range(tiles_w(n))]
        w_banks = [b[:, :, :].rearrange("p a b -> p (a b)") for b in ps_qk] + [b[:, :] for b in ps_num]

        def w_bank(n):
            return w_banks[n % len(w_banks)].rearrange("p (a b) -> p a b", b=wnames[w_tiles[n][0]][2])

        flat = {"q": qt[:, 0:2, :], "k": qt[:, 2:4, :], "v": kt[:, 0:2, :], "g": kt[:, 2:4, :], "o": at[0][:, :, :],
                "fk": at[1][:, 0:4, :], "fr": at[1][:, 4:8, :], "fv": y[:, :].rearrange("p (a b) -> p a b", a=4)}

        def w_stage(name):
            C = wnames[name][0].shape[1]
            return flat[name].rearrange("p a b -> p (a b)").rearrange("p (r c) -> p r c", c=C)

        def w_dram(name):
            return wnames[name][0].rearrange("(r p) c -> p r c", p=P)

        block = ctx.enter_context(nc.Block())

        @block.sync
        def _(sp):
            sp.dma_start(xin[:, :, :], x_g[0]).then_inc(s_x, 16)
            sp.dma_start(w_stage("fk"), w_dram("fk")).then_inc(s_wload["fk"], 16)
            for mu, vector in ((mur, mu_r), (muk, mu_k)):
                sp.dma_start(mu[:, :], vector.rearrange("(k p) -> p k", p=P), allow_slow_non_contiguous=True).then_inc(s_mu, 16)
            for name in setup_w[1:3]:
                sp.dma_start(w_stage(name), w_dram(name)).then_inc(s_wload[name], 16)
            sp.dma_start(gl[:, :], decay_log[None, :].to_broadcast((P, H))).then_inc(s_decay, 16)
            for e in range(2):
                sp.dma_start(gpl[64 * e:64 * e + 64, :], decay_log.rearrange("(p e) -> e p", e=2)[e:e + 1, :].to_broadcast((64, PT)),
                             allow_slow_non_contiguous=True).then_inc(s_decay, 16)
            sp.dma_start(bias[:, :], b_G[None, :].to_broadcast((P, HD))).then_inc(s_bias, 16)

            def group(ap, g):
                return ap[g] if isinstance(g, int) else ap[bass.ds(g, 1)].rearrange("g p c d -> p (g c) d")

            def body(st):
                if st.has("A") and st.before < N - 1:
                    g, p, _ = st.g("A")
                    sp.wait_ge(s_res, 2 * (st.job("A") + 1))
                    sp.dma_start(xin[:, :, :], group(x_g, g + 1)).then_inc(s_x, 16)
                if st.has("C"):
                    g, p, _ = st.g("C")
                    sp.wait_ge(s_res, 2 * (st.job("C") + 1))
                    sp.dma_start(group(out_g, g), x2[p][:, :, :]).then_inc(s_out[p], 16)

            steps(sp, body)
            for p in range(2):
                sp.wait_ge(s_out[p], 16 * (N // 2))

        @block.gpsimd
        def _(pool):
            pool.memset(ident[:, :], 0.0).then_inc(s_ident, 1)
            pool.wait_ge(s_ident, 1)
            pool.affine_select(out=ident[:, :], in_=ident[:, :], compare_op=ALU.not_equal, fill=1.0,
                               base=0, pattern=[[-1, P]], channel_multiplier=1).then_inc(s_ident, 1)
            for t, value in ((zero, 0.0), (m_half, -0.5), (m_one, -1.0), (ln_eps, LN_EPS)):
                pool.memset(t[:, :], value).then_inc(s_const, 1)
            pool.wait_ge(s_const, 4)

            def clear():
                pool.memset(power[:, :, 0:1], 1.0).then_inc(s_const, 1)
                for b in range(2):
                    pool.memset(S[b][:, :, :], 0.0).then_inc(s_const, 1)
                    pool.memset((qh, ql)[b][:, :, :, :].bitcast(F32), 0.0).then_inc(s_const, 1)
                pool.memset(vv[:, :, :, DK:V1], 1.0).then_inc(s_const, 1)

            def rstd(key, mv, rs, nm, n):
                pool.wait_ge(s_var[key], n + 1)
                pool.tensor_tensor(rs[:, :], mv[:, :, 1], ln_eps[:, :], ALU.add).then_inc(s_rv[key], 1)
                pool.tensor_tensor(nm[:, :], mv[:, :, 0], m_one[:, :], ALU.mult).then_inc(s_rv[key], 1)
                pool.wait_ge(s_rv[key], 3 * n + 1)
                pool.tensor_tensor(rs[:, :], rs[:, :], m_half[:, :], ALU.pow).then_inc(s_rv[key], 1)
                pool.wait_ge(s_rv[key], 3 * n + 3)
                pool.tensor_tensor(nm[:, :], nm[:, :], rs[:, :], ALU.mult).then_inc(s_rstd[key], 1)

            def decay_q(st, c):
                g, _, _ = st.g("B")
                if st.before == 1:
                    pool.wait_ge(s_setup, 1)
                pool.wait_ge(s_phi, 8 * g + 4)
                pool.wait_ge(s_num, 8 * g + 2 * c - 2 if c >= 2 else 8 * g)
                pool.tensor_tensor(qd[c % 2][:, :, :], qt[:, :, c * P:(c + 1) * P], qdec[:, :, :], ALU.mult).then_inc(s_qd, 1)

            def q_low(st, c):
                g, _, _ = st.g("B")
                pool.wait_ge(s_qh, 4 * g + c + 1)
                for e in range(2):
                    rows = slice(64 * e, 64 * e + 64)
                    pool.tensor_tensor(ql[rows, :, e, :], qt[rows, :, c * P:(c + 1) * P],
                                       qh[rows, :, e, :].bitcast(F32), ALU.subtract).then_inc(s_ql, 1)
                    pool.wait_ge(s_ql, 8 * g + 2 * c + e + 1)

            def decay_k(st, d):
                g, _, _ = st.g("B")
                if st.before == 1:
                    pool.wait_ge(s_setup, 1)
                pool.wait_ge(s_kh, 4 * g + d + 1)
                pool.tensor_tensor(kl[:, d, :], kt[:, d, :], kh[:, d, :].bitcast(F32), ALU.subtract).then_inc(s_kl, 1)
                pool.wait_ge(s_kl, 4 * g + d + 1)
                k = kt[:, d, :].rearrange("p (c t) -> p c t", t=P)
                pool.tensor_tensor(k, k, kdec[:, d:d + 1, :].to_broadcast((P, CH, P)), ALU.mult).then_inc(s_kdec, 1)

            def mix_low(st, s):
                J = st.job(s)
                pool.wait_ge(s_rsig, 2 * J)
                for k in range(KT):
                    pool.wait_ge(s_mixh["r"], KT * J + k + 1)
                    pool.tensor_tensor(mixl["r"][:, k, :], mix["r"][:, k, :], mixh["r"][:, k, :].bitcast(F32), ALU.subtract).then_inc(s_mixl["r"], 1)

            def body(st):
                a, b, c = st.has("A"), st.has("B"), st.has("C")
                first = st.before == 0
                more = st.before < N - 1
                if first:
                    rstd("f", mv_f, rs_f, nm_f, 0)
                if a:
                    mix_low(st, "A")
                if b:
                    decay_q(st, 0)
                    q_low(st, 0)
                    decay_k(st, 0)
                    decay_k(st, 1)
                if c:
                    rstd("f", mv_f, rs_f, nm_f, st.job("C"))
                if b:
                    decay_k(st, 2)
                    decay_k(st, 3)
                    decay_q(st, 1)
                    q_low(st, 1)
                if first:
                    clear()
                if a:
                    rstd("b", mv_b, rs_b, nm_b, st.g("A")[0])
                if b:
                    q_low(st, 2)
                    decay_q(st, 2)
                if c:
                    mix_low(st, "C")
                if b:
                    q_low(st, 3)
                    decay_q(st, 3)
                if a and more:
                    rstd("f", mv_f, rs_f, nm_f, next_a(st))

            steps(pool, body)

        @block.scalar
        def _(act):
            for name in setup_w[3:]:
                act.dma_start(w_stage(name), w_dram(name)).then_inc(s_wload[name], 16)

            def weights_high(n):
                name, t = w_tiles[n]
                act.wait_ge(s_wt, n + 1)
                act.activation(w_tile(wh[name], t), w_bank(n), ACT.Copy).then_inc(s_wh, 1)

            def decays():
                act.wait_ge(s_decay, 48)
                act.activation(gam[:, :], gl[:, :], ACT.Sigmoid).then_inc(s_gam, 1)
                act.activation(gamp[:, :], gpl[:, :], ACT.Sigmoid).then_inc(s_gam, 1)

            def ln_scale(key, src, rs, nm, xn, n):
                act.wait_ge(s_rstd[key], n + 1)
                for c in range(CH):
                    last = act.activation(xn[:, c, :], src[:, c, :], ACT.Identity, bias=nm[:, c:c + 1], scale=rs[:, c:c + 1])
                last.then_inc(s_xn[key], 1)

            def scale_next_a(st):
                n = next_a(st)
                act.wait_ge(s_xt, 2 * n)
                ln_scale("f", xin, rs_f, nm_f, xn_f, n)

            def scale_c(st):
                _, p, _ = st.g("C")
                act.wait_ge(s_xt, 2 * st.job("C"))
                ln_scale("f", x2[p], rs_f, nm_f, xn_f, st.job("C"))

            def scale_b(st):
                g, p, _ = st.g("A")
                act.wait_ge(s_ks, KT * next_a(st))
                ln_scale("b", x1[p], rs_b, nm_b, xn_b, g)

            def x_high(st, k):
                g, _, _ = st.g("B")
                src = ring[st.tile("B", "xt", k)[0]]
                act.wait_ge(*filled(st, "B", "xt", k))
                if st.before == 1:
                    act.wait_ge(s_const, 10)
                act.wait_ge(s_gpre, 4 * g)
                act.activation(xth[:, k, :], src[:, :], ACT.Copy).then_inc(s_xth, 1)

            def x_turned(st, s, k):
                J = st.job(s)
                _, p, _ = st.g(s)
                src = ring[st.tile(s, "xt", k)[0]]
                act.wait_ge(*filled(st, s, "xt", k))
                act.wait_ge(s_mix["r"], KT * J)
                act.wait_ge(s_mix["k"], KT * J)
                n = 2 * (KT * J + k)
                act.wait_ge(s_carry, n)
                before = zero[:, :] if p == 0 else carry[s][:, k, :]
                act.activation(xt[:, k, 0:1], before, ACT.Copy).then_inc(s_carry, 1)
                act.wait_ge(s_carry, n + 1)
                act.activation(carry[s][:, k, :], src[:, GT - 1:GT], ACT.Copy).then_inc(s_carry, 1)
                act.wait_ge(s_carry, n + 2)
                act.activation(xt[:, k, 1:GT + 1], src[:, :], ACT.Copy).then_inc(s_xt, 1)

            def exp(st, kind, d):
                g, _, _ = st.g("B")
                n = d + (4 if kind == "k" else 0)
                src = ring[st.tile("B", kind, d)[0]]
                act.wait_ge(*filled(st, "B", kind, d))
                if st.before > 1 or n > 1:
                    act.wait_ge(s_phi, 8 * g + n - 1)
                act.activation(ex[n % 2][:, :], src[:, :], ACT.Relu, scale=-1.0).then_inc(s_neg, 1)
                act.wait_ge(s_neg, 8 * g + n + 1)
                act.activation(ex[n % 2][:, :], ex[n % 2][:, :], ACT.Exp, scale=-1.0).then_inc(s_ex, 1)

            def mix_high(st, s, m):
                J = st.job(s)
                act.wait_ge(s_rsig if m == "r" else s_fo, 2 * J)
                for k in range(KT):
                    act.wait_ge(s_mix[m], KT * J + k + 1)
                    act.activation(mixh[m][:, k, :], mix[m][:, k, :], ACT.Copy).then_inc(s_mixh[m], 1)

            def k_high(st, d):
                g, _, _ = st.g("B")
                act.wait_ge(s_phi, 8 * g + 4 + d + 1)
                act.wait_ge(s_qk, 8 * g)
                act.activation(kh[:, d, :], kt[:, d, :], ACT.Copy).then_inc(s_kh, 1)

            def q_high(st, c):
                g, _, _ = st.g("B")
                act.wait_ge(s_phi, 8 * g + 4)
                act.wait_ge(s_qk, 8 * g + 2 * c)
                for e in range(2):
                    rows = slice(64 * e, 64 * e + 64)
                    last = act.activation(qh[rows, :, e, :], qt[rows, :, c * P:(c + 1) * P], ACT.Copy)
                last.then_inc(s_qh, 1)

            def relu(st, s, d):
                J = st.job(s)
                src = ring[st.tile(s, "k", d)[0]]
                act.wait_ge(*filled(st, s, "k", d))
                act.wait_ge(s_mix["k"], KT * (J + 1))
                act.wait_ge(s_mix["r"], KT * (J + 1))
                act.activation(kr[:, d, :], src[:, :], ACT.Relu).then_inc(s_kr, 1)

            def square_high(st, s):
                J = st.job(s)
                act.wait_ge(s_kr, KT * (J + 1))
                for d in range(KT):
                    act.wait_ge(s_ks, KT * J + d + 1)
                    act.activation(ksh[:, d, :], ks[:, d, :], ACT.Copy).then_inc(s_ksh, 1)

            def sigmoid_r(st, s, t):
                J = st.job(s)
                src = ring[st.tile(s, "r", t)[0]]
                act.wait_ge(*filled(st, s, "r", t))
                act.wait_ge(s_mixl["r"], KT * (J + 1))
                act.activation(rsig[:, 2 * t:2 * t + 2, :], src[:, :].rearrange("p (c d) -> p c d", c=2), ACT.Sigmoid).then_inc(s_rsig, 1)

            def values(st, c):
                g, _, _ = st.g("B")
                src = ring[st.tile("B", "v", c)[0]]
                act.wait_ge(*filled(st, "B", "v", c))
                if c >= 2 or st.before > 1:
                    act.wait_ge(s_num, 8 * g + 2 * c - 2)
                    act.wait_ge(s_S, 8 * g + 2 * c - 2)
                act.activation(vv[:, c % 2, :, 0:DK], src[:, :].rearrange("p (h e) -> p h e", h=H), ACT.Copy).then_inc(s_vv, 1)

            def decayed_k(st, c):
                g, _, _ = st.g("B")
                src = ring[st.tile("B", "kt", c)[0]]
                act.wait_ge(*filled(st, "B", "kt", c))
                if c >= 2 or st.before > 1:
                    act.wait_ge(s_S, 8 * g + 2 * c - 2)
                act.activation(kd[c % 2][:, :], src[:, :], ACT.Copy).then_inc(s_kd, 1)

            def sigmoid_gate(st, c):
                g, _, _ = st.g("B")
                act.wait_ge(s_gpre, 4 * g + c + 1)
                act.activation(gate[:, c % 2, :], gate[:, c % 2, :], ACT.Sigmoid).then_inc(s_gate, 1)

            def y_high(st, c):
                g, _, _ = st.g("B")
                src = ring[st.tile("B", "yt", c)[0]]
                act.wait_ge(*filled(st, "B", "yt", c))
                act.wait_ge(s_x2, 2 * g + c // 2)
                act.activation(yh[c % 2][:, :, :], src[:, :].rearrange("p (d t) -> p d t", t=P), ACT.Copy).then_inc(s_yh, 1)

            def body(st):
                a, b, c = st.has("A"), st.has("B"), st.has("C")
                first = st.before == 0
                more = st.before < N - 1
                if first:
                    ln_scale("f", xin, rs_f, nm_f, xn_f, 0)
                if b:
                    x_high(st, 0)
                if first:
                    weights_high(0)
                if b:
                    x_high(st, 1)
                if a:
                    x_turned(st, "A", 0)
                    x_turned(st, "A", 1)
                if b:
                    exp(st, "q", 0)
                    exp(st, "q", 1)
                if a:
                    mix_high(st, "A", "k")
                if b:
                    exp(st, "q", 2)
                if a:
                    mix_high(st, "A", "r")
                if b:
                    exp(st, "q", 3)
                    exp(st, "k", 0)
                    q_high(st, 0)
                    exp(st, "k", 1)
                if first:
                    weights_high(1)
                    weights_high(2)
                    weights_high(3)
                if b:
                    k_high(st, 0)
                if a:
                    relu(st, "A", 0)
                if b:
                    exp(st, "k", 2)
                    k_high(st, 1)
                    exp(st, "k", 3)
                if first:
                    weights_high(4)
                if a:
                    relu(st, "A", 1)
                if b:
                    k_high(st, 2)
                if a:
                    square_high(st, "A")
                    sigmoid_r(st, "A", 0)
                    sigmoid_r(st, "A", 1)
                if first:
                    weights_high(5)
                if b:
                    k_high(st, 3)
                    values(st, 0)
                if c:
                    scale_c(st)
                if first:
                    weights_high(6)
                    decays()
                if b:
                    values(st, 1)
                if c:
                    x_turned(st, "C", 0)
                if b:
                    sigmoid_gate(st, 0)
                if c:
                    x_turned(st, "C", 1)
                if b:
                    q_high(st, 1)
                if first:
                    weights_high(7)
                if b:
                    decayed_k(st, 0)
                    decayed_k(st, 1)
                if c:
                    mix_high(st, "C", "r")
                if b:
                    q_high(st, 2)
                    y_high(st, 0)
                    values(st, 2)
                    sigmoid_gate(st, 1)
                if first:
                    weights_high(8)
                if b:
                    sigmoid_gate(st, 2)
                if c:
                    mix_high(st, "C", "k")
                if b:
                    q_high(st, 3)
                if c:
                    relu(st, "C", 0)
                    relu(st, "C", 1)
                if first:
                    weights_high(9)
                if b:
                    y_high(st, 1)
                    decayed_k(st, 2)
                if c:
                    square_high(st, "C")
                if b:
                    sigmoid_gate(st, 3)
                if a:
                    scale_b(st)
                if b:
                    values(st, 3)
                    y_high(st, 2)
                if c:
                    sigmoid_r(st, "C", 0)
                if first:
                    weights_high(10)
                    weights_high(11)
                if c:
                    sigmoid_r(st, "C", 1)
                if first:
                    weights_high(12)
                if b:
                    decayed_k(st, 3)
                    y_high(st, 3)
                if a and more:
                    scale_next_a(st)

            steps(act, body)

        @block.vector
        def _(dve):
            def ln_stats(key, src, st_, mv, n):
                if isinstance(n, int) and n == 0 and key == "f":
                    dve.wait_ge(s_x, 16)
                for c in range(CH):
                    last = dve.bn_stats(st_[:, c, :], src[:, c, :])
                last.then_inc(s_stat[key], 1)
                dve.wait_ge(s_stat[key], n + 1)
                dve.memset(spare[:, :], 0.0)
                for c in range(CH):
                    last = dve.bn_aggr(mv[:, c, :], st_[:, c, :])
                last.then_inc(s_var[key], 1)

            def weights_low(n):
                name, t = w_tiles[n]
                dve.wait_ge(s_wh, n + 1)
                dve.tensor_tensor(w_tile(wl[name], t), w_bank(n), w_tile(wh[name], t).bitcast(F32), ALU.subtract).then_inc(s_wl, 1)

            def decay_tables():
                dve.wait_ge(s_gam, 2)
                dve.wait_ge(s_ident, 2)
                dve.wait_ge(s_const, 10)
                for h in range(H):
                    dve.tensor_tensor_scan(dmask[:, h, :], gam[:, h:h + 1].to_broadcast((P, P)), ident[:, :], 0.0, ALU.mult, ALU.add)
                for d in range(PT):
                    last = dve.tensor_tensor_scan(qdec[:, d, :], gamp[:, d:d + 1].to_broadcast((P, P)), S[0][:, 0, 0:P], 1.0, ALU.mult, ALU.add)
                last.then_inc(s_setup, 1)
                dve.wait_ge(s_setup, 1)

            def stats_next_a(st):
                g, p, h = st.g("A", 1)
                dve.wait_ge(s_x, 16 * (g + 1))
                ln_stats("f", xin, st_f, mv_f, next_a(st))

            def stats_c(st):
                g, p, h = st.g("C")
                dve.wait_ge(s_x2, 2 * (g + 1))
                ln_stats("f", x2[p], st_f, mv_f, st.job("C"))

            def stats_b(st):
                g, p, h = st.g("A")
                dve.wait_ge(s_res, 2 * (st.job("A") + 1))
                ln_stats("b", x1[p], st_b, mv_b, g)

            def residual(st, s, t):
                J = st.job(s)
                g, p, h = st.g(s)
                src, dst = (xin, x1[p]) if s == "A" else (x2[p], x2[p])
                dve.wait_ge(s_fo, 2 * J + t + 1)
                if t == 0 and s == "A" and st.before >= 2:
                    dve.wait_ge(s_x2, 2 * (g - 1))
                dve.tensor_tensor(dst[:, 2 * t:2 * t + 2, :], src[:, 2 * t:2 * t + 2, :],
                                   fo[:, 2 * t:2 * t + 2, :], ALU.add).then_inc(s_res, 1)

            def x_low(st, k):
                g, _, _ = st.g("B")
                src = ring[st.tile("B", "xt", k)[0]]
                dve.wait_ge(*filled(st, "B", "xt", k))
                dve.wait_ge(s_xth, 2 * g + k + 1)
                dve.tensor_tensor(xtl[:, k, :], src[:, :], xth[:, k, :].bitcast(F32), ALU.subtract).then_inc(s_xtl, 1)

            def shift_difference(st, s):
                J = st.job(s)
                dve.wait_ge(s_ks, KT * J)
                if st.has("B"):
                    dve.wait_ge(s_xth, 2 * (st.g("B")[0] + 1))
                for k in range(KT):
                    dve.wait_ge(s_xt, KT * J + k + 1)
                    dve.tensor_tensor(dx[:, k, :], xt[:, k, 1:GT + 1], xt[:, k, 0:GT], ALU.subtract).then_inc(s_dx, 1)

            def mixes(st, s, m):
                J = st.job(s)
                _, p, _ = st.g(s)
                mu = muk if m == "k" else mur
                if st.before == 0:
                    dve.wait_ge(s_mu, 32)
                if m == "k":
                    dve.wait_ge(s_ksh, KT * J)
                    dve.wait_ge(s_ksl, KT * J)
                else:
                    dve.wait_ge(s_res, 2 * J)
                for k in range(KT):
                    dve.wait_ge(s_dx, KT * J + k + 1)
                    dve.scalar_tensor_tensor(mix[m][:, k, :], dx[:, k, :], mu[:, k:k + 1], xt[:, k, 0:GT],
                                             ALU.mult, ALU.add).then_inc(s_mix[m], 1)

            def mix_low(st, s):
                J = st.job(s)
                for k in range(KT):
                    dve.wait_ge(s_mixh["k"], KT * J + k + 1)
                    dve.tensor_tensor(mixl["k"][:, k, :], mix["k"][:, k, :], mixh["k"][:, k, :].bitcast(F32), ALU.subtract).then_inc(s_mixl["k"], 1)

            def phi(st, kind, d):
                g, _, _ = st.g("B")
                n = d + (4 if kind == "k" else 0)
                src = ring[st.tile("B", kind, d)[0]]
                dve.wait_ge(*filled(st, "B", kind, d))
                dve.wait_ge(s_ex, 8 * g + n + 1)
                if n == 0:
                    dve.wait_ge(s_qk, 8 * g)
                    dve.wait_ge(s_qd, 4 * g)
                if n == 4:
                    dve.wait_ge(s_kdec, 4 * g)
                    dve.wait_ge(s_kd, 4 * g)
                dst = qt if kind == "q" else kt
                dve.scalar_tensor_tensor(dst[:, d, :], src[:, :], 1.0, ex[n % 2][:, :], ALU.add, ALU.max).then_inc(s_phi, 1)

            def square(st, s, d):
                J = st.job(s)
                src = ring[st.tile(s, "k", d)[0]]
                dve.wait_ge(*filled(st, s, "k", d))
                dve.wait_ge(s_kr, 2 * J + d + 1)
                dve.wait_ge(s_mixh["k"], KT * (J + 1))
                dve.wait_ge(s_mixl["k"], KT * (J + 1))
                dve.tensor_tensor(ks[:, d, :], src[:, :], kr[:, d, :], ALU.mult).then_inc(s_ks, 1)

            def square_low(st, s):
                J = st.job(s)
                for d in range(KT):
                    dve.wait_ge(s_ksh, KT * J + d + 1)
                    dve.tensor_tensor(ksl[:, d, :], ks[:, d, :], ksh[:, d, :].bitcast(F32), ALU.subtract).then_inc(s_ksl, 1)

            def mask_scores(st, c):
                g, _, _ = st.g("B")
                for half in range(2):
                    dve.wait_ge(s_qk, 8 * g + 2 * c + half + 1)
                    if half == 0 and c >= 2:
                        dve.wait_ge(s_num, 8 * g + 2 * c - 2)
                    dve.tensor_tensor(at[c % 2][:, 4 * half:4 * half + 4, :], ps_qk[half][:, :, :],
                                      dmask[:, 4 * half:4 * half + 4, :], ALU.mult).then_inc(s_at, 1)

            def gate_bias(st, c):
                g, _, _ = st.g("B")
                src = ring[st.tile("B", "g", c)[0]]
                if st.before == 1:
                    dve.wait_ge(s_bias, 16)
                dve.wait_ge(*filled(st, "B", "g", c))
                dve.wait_ge(s_y, 8 * g + 2 * c - 2 if c >= 2 else 8 * g)
                dve.tensor_tensor(gate[:, c % 2, :], src[:, :], bias[:, :], ALU.add).then_inc(s_gpre, 1)

            def state(st, c):
                g, p, _ = st.g("B")
                dve.wait_ge(s_num, 8 * g + 2 * c)
                for r in range(2):
                    src = ring[st.tile("B", "s", 2 * c + r)[0]]
                    dve.wait_ge(*filled(st, "B", "s", 2 * c + r))
                    dve.wait_ge(s_S, 8 * g + 2 * c)
                    for d in (2 * r, 2 * r + 1):
                        for e in range(2):
                            rows, cols = slice(64 * e, 64 * e + 64), slice(V1 * e, V1 * e + V1)
                            at_ps = 2 * V1 * (d - 2 * r) + V1 * e
                            new, got = S[(c + 1) % 2][rows, d, cols], src[rows, at_ps:at_ps + V1]
                            if p == 0 and c == 0:
                                last = dve.tensor_copy(new, got)
                            else:
                                last = dve.scalar_tensor_tensor(new, S[c % 2][rows, d, cols], qdec[rows, d, P - 1:P], got,
                                                                ALU.mult, ALU.add)
                    last.then_inc(s_S, 1)

            def outputs(st, c):
                g, _, _ = st.g("B")
                for half in range(2):
                    dve.wait_ge(s_num, 8 * g + 2 * c + half + 1)
                    num = ps_num[half][:, 0:4 * V1].rearrange("p (h e) -> p h e", e=V1)
                    dve.tensor_scalar(den[:, 4 * half:4 * half + 4], num[:, :, DK], DEN_EPS, None, ALU.add).then_inc(s_den, 1)
                    dve.wait_ge(s_den, 8 * g + 2 * c + half + 1)
                    dve.reciprocal(rden[:, 4 * half:4 * half + 4], den[:, 4 * half:4 * half + 4]).then_inc(s_rden, 1)
                    dve.wait_ge(s_rden, 8 * g + 2 * c + half + 1)
                    dve.wait_ge(s_gate, 4 * g + c + 1)
                    dve.wait_ge(s_yl, 4 * g + c)
                    for h in range(4 * half, 4 * half + 4):
                        last = dve.scalar_tensor_tensor(y[:, h * DK:(h + 1) * DK], num[:, h % 4, 0:DK], rden[:, h:h + 1],
                                                        gate[:, c % 2, h * DK:(h + 1) * DK], ALU.mult, ALU.mult)
                    last.then_inc(s_y, 1)

            def y_low(st, c):
                g, _, _ = st.g("B")
                src = ring[st.tile("B", "yt", c)[0]]
                dve.wait_ge(*filled(st, "B", "yt", c))
                dve.wait_ge(s_yh, 4 * g + c + 1)
                dve.wait_ge(s_x2, 2 * g + c // 2)
                dve.tensor_tensor(yl[c % 2][:, :, :], src[:, :].rearrange("p (d t) -> p d t", t=P),
                                  yh[c % 2][:, :, :].bitcast(F32), ALU.subtract).then_inc(s_yl, 1)

            def residual_b(st, t):
                g, p, h = st.g("B")
                src = ring[st.tile("B", "o", t)[0]]
                dve.wait_ge(*filled(st, "B", "o", t))
                dve.wait_ge(s_out[p], 16 * h)
                dve.tensor_tensor(x2[p][:, 2 * t:2 * t + 2, :], src[:, :].rearrange("p (c d) -> p c d", c=2),
                                  x1[p][:, 2 * t:2 * t + 2, :], ALU.add).then_inc(s_x2, 1)

            def gated(st, s, t):
                J = st.job(s)
                src = ring[st.tile(s, "kv", t)[0]]
                dve.wait_ge(*filled(st, s, "kv", t))
                dve.wait_ge(s_rsig, 2 * J + t + 1)
                dve.scalar_tensor_tensor(fo[:, 2 * t:2 * t + 2, :], src[:, :].rearrange("p (c d) -> p c d", c=2), 0.5,
                                         rsig[:, 2 * t:2 * t + 2, :], ALU.mult, ALU.mult).then_inc(s_fo, 1)


            def body(st):
                a, b, c = st.has("A"), st.has("B"), st.has("C")
                first = st.before == 0
                more = st.before < N - 1
                if b:
                    x_low(st, 0)
                if first:
                    ln_stats("f", xin, st_f, mv_f, 0)
                    weights_low(0)
                if b:
                    x_low(st, 1)
                if a:
                    shift_difference(st, "A")
                    mixes(st, "A", "k")
                    mixes(st, "A", "r")
                if b:
                    phi(st, "q", 0)
                    phi(st, "q", 1)
                    gate_bias(st, 0)
                if a:
                    mix_low(st, "A")
                if b:
                    phi(st, "q", 2)
                    phi(st, "q", 3)
                    gate_bias(st, 1)
                if first:
                    weights_low(1)
                if b:
                    phi(st, "k", 0)
                if first:
                    weights_low(2)
                if c:
                    stats_c(st)
                if b:
                    phi(st, "k", 1)
                if a:
                    square(st, "A", 0)
                if first:
                    weights_low(3)
                if b:
                    phi(st, "k", 2)
                if a:
                    square(st, "A", 1)
                if b:
                    phi(st, "k", 3)
                if a:
                    square_low(st, "A")
                if first:
                    weights_low(4)
                if a:
                    gated(st, "A", 0)
                    residual(st, "A", 0)
                    gated(st, "A", 1)
                    residual(st, "A", 1)
                    stats_b(st)
                if b:
                    mask_scores(st, 0)
                if c:
                    shift_difference(st, "C")
                if first:
                    weights_low(5)
                if c:
                    mixes(st, "C", "r")
                if b:
                    outputs(st, 0)
                    gate_bias(st, 2)
                    state(st, 0)
                    mask_scores(st, 1)
                if c:
                    mixes(st, "C", "k")
                if b:
                    state(st, 1)
                if first:
                    weights_low(6)
                if b:
                    y_low(st, 0)
                if c:
                    mix_low(st, "C")
                if first:
                    weights_low(7)
                if b:
                    outputs(st, 1)
                    mask_scores(st, 2)
                if c:
                    square(st, "C", 0)
                if b:
                    gate_bias(st, 3)
                    y_low(st, 1)
                if c:
                    square(st, "C", 1)
                if a and more:
                    stats_next_a(st)
                if first:
                    weights_low(8)
                if b:
                    outputs(st, 2)
                if first:
                    weights_low(9)
                if b:
                    residual_b(st, 0)
                if first:
                    weights_low(10)
                if b:
                    mask_scores(st, 3)
                    state(st, 2)
                if c:
                    square_low(st, "C")
                if b:
                    y_low(st, 2)
                    outputs(st, 3)
                    y_low(st, 3)
                if first:
                    weights_low(11)
                if c:
                    gated(st, "C", 0)
                    residual(st, "C", 0)
                if first:
                    weights_low(12)
                    decay_tables()
                if b:
                    state(st, 3)
                if c:
                    gated(st, "C", 1)
                    residual(st, "C", 1)
                if b:
                    residual_b(st, 1)

            steps(dve, body)

        @block.tensor
        def _(pe):
            pe.wait_ge(s_ident, 2)

            def turn_weights(n):
                name, t = w_tiles[n]
                pe.wait_ge(s_wload[name], 16)
                if n >= len(w_banks):
                    pe.wait_ge(s_wl, n - len(w_banks) + 1)
                for z in range(4):
                    kk, r = (t, z) if wnames[name][2] == GT else (2 * t + z // 2, z % 2)
                    last = pe.transpose(w_banks[n % 4][:, z * P:(z + 1) * P], w_stage(name)[:, r, kk * P:(kk + 1) * P], ident[:, :])
                last.then_inc(s_wt, 1)

            def three_passes(out, lhs, rhs, first=True, last=True):
                (lh, ll), (rh, rl) = lhs, rhs
                pe.matmul(out, ll, rh, start=first, stop=False)
                pe.matmul(out, lh, rl, start=False, stop=False)
                return pe.matmul(out, lh, rh, start=False, stop=last)

            def turn(st, s, k):
                xn, key = (xn_b, "b") if s == "B" else (xn_f, "f")
                n = st.g("B")[0] if s == "B" else st.job(s)
                if s == "B" and st.before == 1:
                    pe.wait_ge(s_wl, len(w_tiles))
                pe.wait_ge(s_xn[key], n + 1)
                pe.wait_ge(*emptied(st, s, "xt", k))
                b, _ = st.tile(s, "xt", k)
                for c in range(CH):
                    last = pe.transpose(ring[b][:, c * P:(c + 1) * P], xn[:, c, k * P:(k + 1) * P], ident[:, :])
                last.then_inc(ready[b], 1)

            def project(st, kind, d):
                g, _, _ = st.g("B")
                pe.wait_ge(*emptied(st, "B", kind, d))
                b, _ = st.tile("B", kind, d)
                cols = slice(d * P, (d + 1) * P)
                for k in range(KT):
                    if kind == "q" and d == 0:
                        pe.wait_ge(s_xtl, 2 * g + k + 1)
                    last = three_passes(ring[b][:, :], (wh[kind][:, k, cols], wl[kind][:, k, cols]),
                                        (xth[:, k, :], xtl[:, k, :]), k == 0, k == KT - 1)
                last.then_inc(ready[b], 1)

            def project_tokens(st, kind, c):
                pe.wait_ge(*emptied(st, "B", kind, c))
                b, _ = st.tile("B", kind, c)
                cols = slice(c * P, (c + 1) * P)
                for k in range(KT):
                    last = three_passes(ring[b][:, :], (xth[:, k, cols], xtl[:, k, cols]),
                                        (wh[kind][:, k, :], wl[kind][:, k, :]), k == 0, k == KT - 1)
                last.then_inc(ready[b], 1)

            def turn_k(st, c):
                g, _, _ = st.g("B")
                pe.wait_ge(s_kdec, 4 * (g + 1))
                pe.wait_ge(*emptied(st, "B", "kt", c))
                b, _ = st.tile("B", "kt", c)
                for d in range(PT):
                    last = pe.transpose(ring[b][:, d * P:(d + 1) * P], kt[:, d, c * P:(c + 1) * P], ident[:, :])
                last.then_inc(ready[b], 1)

            def scores(st, c):
                g, _, _ = st.g("B")
                pe.wait_ge(s_kl, 4 * (g + 1))
                pe.wait_ge(s_ql, 8 * g + 2 * c + 2)
                for half in range(2):
                    pe.wait_ge(s_at, 8 * g + 2 * c + half - 1 if c + half else 8 * g)
                    for dd in range(2):
                        d = 2 * half + dd
                        last = three_passes(ps_qk[half][:, 2 * dd:2 * dd + 2, :].rearrange("p e t -> p (e t)"),
                                            (kh[:, d, c * P:(c + 1) * P], kl[:, d, c * P:(c + 1) * P]),
                                            (qh[:, d, :, :].rearrange("p e t -> p (e t)"), ql[:, d, :, :].rearrange("p e t -> p (e t)")))
                    last.then_inc(s_qk, 1)

            def state_products(st, c, r):
                g, _, _ = st.g("B")
                pe.wait_ge(s_kd, 4 * g + c + 1)
                pe.wait_ge(s_vv, 4 * g + c + 1)
                pe.wait_ge(*emptied(st, "B", "s", 2 * c + r))
                b, _ = st.tile("B", "s", 2 * c + r)
                for d in (2 * r, 2 * r + 1):
                    last = pe.matmul(ring[b][:, 2 * V1 * (d - 2 * r):2 * V1 * (d - 2 * r + 1)], kd[c % 2][:, d * P:(d + 1) * P],
                                     vv[:, c % 2, 2 * d:2 * d + 2, :].rearrange("p h e -> p (h e)"), start=True, stop=True)
                last.then_inc(ready[b], 1)

            def numerators(st, c):
                g, p, _ = st.g("B")
                fresh = p == 0 and c == 0
                pe.wait_ge(s_vv, 4 * g + c + 1)
                for half in range(2):
                    pe.wait_ge(s_at, 8 * g + 2 * c + half + 1)
                    pe.wait_ge(s_y, 8 * g + 2 * c + half - 1 if c + half else 8 * g)
                    pe.wait_ge(s_qd, 4 * g + c + 1)
                    if not fresh:
                        pe.wait_ge(s_S, 8 * g + 2 * c)
                    for dd in range(2):
                        d = 2 * half + dd
                        at_ps = 2 * V1 * dd
                        if not fresh:
                            pe.matmul(ps_num[half][:, at_ps:at_ps + 2 * V1], qd[c % 2][:, d, :], S[c % 2][:, d, :],
                                      start=True, stop=False)
                        for e in range(2):
                            last = pe.matmul(ps_num[half][:, at_ps + V1 * e:at_ps + V1 * e + V1], at[c % 2][:, 2 * d + e, :],
                                             vv[:, c % 2, 2 * d + e, :], start=fresh, stop=fresh or e == 1)
                    last.then_inc(s_num, 1)

            def turn_y(st, c):
                g, _, _ = st.g("B")
                pe.wait_ge(s_y, 8 * g + 2 * c + 2)
                pe.wait_ge(*emptied(st, "B", "yt", c))
                b, _ = st.tile("B", "yt", c)
                for d in range(PT):
                    last = pe.transpose(ring[b][:, d * P:(d + 1) * P], y[:, d * P:(d + 1) * P], ident[:, :])
                last.then_inc(ready[b], 1)

            def project_out(st, t):
                g, _, _ = st.g("B")
                pe.wait_ge(s_yl, 4 * g + 2 * t + 2)
                pe.wait_ge(*emptied(st, "B", "o", t))
                b, _ = st.tile("B", "o", t)
                for z in range(2):
                    for d in range(PT):
                        last = three_passes(ring[b][:, z * D:(z + 1) * D], (yh[z][:, d, :], yl[z][:, d, :]),
                                            (wh["o"][:, d, :], wl["o"][:, d, :]), d == 0, d == PT - 1)
                last.then_inc(ready[b], 1)

            def ffn_k(st, s, d):
                J = st.job(s)
                if st.before == 0:
                    pe.wait_ge(s_wl, w_tiles.index(("fk", 0)) + 1)
                pe.wait_ge(*emptied(st, s, "k", d))
                b, _ = st.tile(s, "k", d)
                cols = slice(d * P, (d + 1) * P)
                for k in range(KT):
                    pe.wait_ge(s_mixl["k"], KT * J + k + 1)
                    last = three_passes(ring[b][:, :], (wh["fk"][:, k, cols], wl["fk"][:, k, cols]),
                                        (mixh["k"][:, k, :], mixl["k"][:, k, :]), k == 0, k == KT - 1)
                last.then_inc(ready[b], 1)

            def ffn_tokens(st, s, kind, t):
                J = st.job(s)
                if kind == "r":
                    pe.wait_ge(s_mixl["r"], KT * (J + 1))
                    xh_, xl_, w = mixh["r"], mixl["r"], "fr"
                else:
                    pe.wait_ge(s_ksl, KT * (J + 1))
                    xh_, xl_, w = ksh, ksl, "fv"
                if st.before == 0:
                    pe.wait_ge(s_wl, w_tiles.index((w, 0)) + 1)
                pe.wait_ge(*emptied(st, s, kind, t))
                b, _ = st.tile(s, kind, t)
                for z in range(2):
                    cols = slice((2 * t + z) * P, (2 * t + z + 1) * P)
                    for k in range(KT):
                        last = three_passes(ring[b][:, z * D:(z + 1) * D], (xh_[:, k, cols], xl_[:, k, cols]),
                                            (wh[w][:, k, :], wl[w][:, k, :]), k == 0, k == KT - 1)
                last.then_inc(ready[b], 1)

            def body(st):
                a, b, c = st.has("A"), st.has("B"), st.has("C")
                first = st.before == 0
                if first:
                    turn_weights(0)
                if b:
                    turn(st, "B", 0)
                    turn(st, "B", 1)
                if a:
                    turn(st, "A", 0)
                    turn(st, "A", 1)
                if first:
                    turn_weights(1)
                if b:
                    project(st, "q", 0)
                    project(st, "q", 1)
                    project_tokens(st, "g", 0)
                    project(st, "q", 2)
                if first:
                    turn_weights(2)
                if b:
                    project(st, "q", 3)
                    project(st, "k", 0)
                if first:
                    turn_weights(3)
                    turn_weights(4)
                if b:
                    project_tokens(st, "g", 1)
                    project(st, "k", 1)
                if a:
                    ffn_k(st, "A", 0)
                if b:
                    project(st, "k", 2)
                    project(st, "k", 3)
                if a:
                    ffn_k(st, "A", 1)
                    ffn_tokens(st, "A", "r", 0)
                    ffn_tokens(st, "A", "r", 1)
                if b:
                    project_tokens(st, "v", 0)
                if a:
                    ffn_tokens(st, "A", "kv", 0)
                    ffn_tokens(st, "A", "kv", 1)
                if b:
                    project_tokens(st, "v", 1)
                if first:
                    turn_weights(5)
                if c:
                    turn(st, "C", 0)
                    turn(st, "C", 1)
                if first:
                    turn_weights(6)
                    turn_weights(7)
                if b:
                    scores(st, 0)
                    turn_k(st, 0)
                    turn_k(st, 1)
                    numerators(st, 0)
                    state_products(st, 0, 0)
                    project_tokens(st, "g", 2)
                    state_products(st, 0, 1)
                    scores(st, 1)
                    project_tokens(st, "v", 2)
                    state_products(st, 1, 0)
                    turn_y(st, 0)
                    state_products(st, 1, 1)
                    numerators(st, 1)
                    scores(st, 2)
                    project_tokens(st, "g", 3)
                if c:
                    ffn_k(st, "C", 0)
                    ffn_k(st, "C", 1)
                if first:
                    turn_weights(8)
                if b:
                    turn_y(st, 1)
                    numerators(st, 2)
                    turn_k(st, 2)
                    project_out(st, 0)
                    state_products(st, 2, 0)
                    scores(st, 3)
                    project_tokens(st, "v", 3)
                    state_products(st, 2, 1)
                if c:
                    ffn_tokens(st, "C", "r", 0)
                if b:
                    turn_y(st, 2)
                    numerators(st, 3)
                if first:
                    turn_weights(9)
                if b:
                    turn_k(st, 3)
                if c:
                    ffn_tokens(st, "C", "r", 1)
                if first:
                    turn_weights(10)
                if b:
                    turn_y(st, 3)
                if first:
                    turn_weights(11)
                if c:
                    ffn_tokens(st, "C", "kv", 0)
                if b:
                    state_products(st, 3, 0)
                if c:
                    ffn_tokens(st, "C", "kv", 1)
                if b:
                    state_products(st, 3, 1)
                    project_out(st, 1)
                if first:
                    turn_weights(12)

            steps(pe, body)


_INS = ["x", "W_Q", "W_K", "W_V", "W_g_w", "W_g_b", "W_O", "decay_log"]
_FFN = ["W_r", "W_k", "W_v", "mu_r", "mu_k"]


def kernel(**inputs):
    import numpy as _np
    import concourse.bacc as _bacc
    from concourse import mybir as _mybir
    from concourse.bass_utils import run_bass_kernel_spmd as _run

    nc = _bacc.Bacc("TRN2", target_bir_lowering=False, num_devices=1)
    arrays, args = {}, []
    for name in ["L0_attn_" + n for n in _INS] + ["L0_ffn_" + n for n in _FFN]:
        a = _np.ascontiguousarray(inputs[name])
        arrays[f"in_{name}_dram"] = a
        args.append(nc.dram_tensor(f"in_{name}_dram", a.shape, _mybir.dt.from_np(a.dtype), kind="ExternalInput").ap())
    shape = inputs["L0_attn_x"].shape
    args.append(nc.dram_tensor("out_0_dram", shape, _mybir.dt.float32, kind="ExternalOutput").ap())
    macaron(nc, *args)
    r = _run(nc, [arrays], core_ids=[0])
    return r.results[0]["out_0_dram"]
```
